# Optimizing a Trainium2 kernel written in Bass

```python
import numpy as np
import jax
import jax.numpy as jnp

def _softmax(x, axis=-1):
    return jax.nn.softmax(x, axis=axis)

def _gelu(x):
    return jax.nn.gelu(x, approximate=True)

def _silu(x):
    return jax.nn.silu(x)

def _sigmoid(x):
    return jax.nn.sigmoid(x)

def _layernorm(x, axis=-1, eps=1e-05):
    m = jnp.mean(x, axis=axis, keepdims=True)
    v = jnp.var(x, axis=axis, keepdims=True)
    return (x - m) / jnp.sqrt(v + eps)

def _scatter_add(tgt, idx, src, axis=0):
    return tgt.at[idx].add(src)

def _segment_sum(src, seg, n):
    return jax.ops.segment_sum(src, seg, n)
kernel_name = 'mk_adaln_d2_jaxref_r4_54f4a7'

def setup_inputs(seed: int=0):
    np.random.seed(seed)
    _w = jnp.asarray

    def _L0_attn_setup():
        import jax, jax.numpy as jnp
        import numpy as np
        import math
        D_MODEL = 256
        N_HEADS = 16
        DH = D_MODEL // N_HEADS
        THETA = 10000.0

        def _rope_tables(S):
            inv_freq = 1.0 / THETA ** (jnp.arange(0, DH, 2, dtype=jnp.float32) / DH)
            ang = jnp.arange(S, dtype=jnp.float32)[:, None] * inv_freq[None, :]
            cos = jnp.concatenate([jnp.cos(ang), jnp.cos(ang)], axis=-1)
            sin = jnp.concatenate([jnp.sin(ang), jnp.sin(ang)], axis=-1)
            return (cos, sin)

        def _apply_rope(x, cos, sin):
            x1, x2 = jnp.split(x, 2, axis=-1)
            rot = jnp.concatenate([-x2, x1], axis=-1)
            c = cos[None, :, None, :]
            s = sin[None, :, None, :]
            return x * c + rot * s
        key = jax.random.key(seed)
        k1, k2, k3 = jax.random.split(key, 3)
        x = jax.random.normal(k1, (4, 512, D_MODEL), dtype=jnp.float32)
        qkv = 0.01 * jax.random.normal(k2, (3 * D_MODEL, D_MODEL), dtype=jnp.float32)
        wo = 0.01 * jax.random.normal(k3, (D_MODEL, D_MODEL), dtype=jnp.float32)
        return {'x': x, 'qkv': qkv, 'wo': wo}
    _L0_attn_in = _L0_attn_setup()

    def _L0_ffn_setup():
        import jax, jax.numpy as jnp
        import numpy as np
        DIM = 256

        def _reference_tuple_inner(x, W_r, W_k, W_v, mu_r, mu_k):
            B, T, C = x.shape
            x_prev = jnp.concatenate([jnp.zeros((B, 1, C), x.dtype), x[:, :-1, :]], axis=1)
            xr = mu_r * x + (1.0 - mu_r) * x_prev
            xk = mu_k * x + (1.0 - mu_k) * x_prev
            r = jax.nn.sigmoid(jnp.einsum('btc,dc->btd', xr, W_r))
            k = jnp.einsum('btc,dc->btd', xk, W_k)
            k_act = jnp.square(jax.nn.relu(k))
            out = r * jnp.einsum('btc,dc->btd', k_act, W_v)
            new_state = x[:, -1, :]
            return (out, new_state)
        key = jax.random.key(seed)
        ks = jax.random.split(key, 6)
        B, T, C = (8, 512, DIM)
        x = jax.random.normal(ks[0], (B, T, C), dtype=jnp.float32)
        s = 1.0 / np.sqrt(C)
        W_r = jax.random.uniform(ks[1], (C, C), jnp.float32, -s, s)
        W_k = jax.random.uniform(ks[2], (C, C), jnp.float32, -s, s)
        W_v = jax.random.uniform(ks[3], (C, C), jnp.float32, -s, s)
        mu_r = jax.random.uniform(ks[4], (C,), jnp.float32)
        mu_k = jax.random.uniform(ks[5], (C,), jnp.float32)
        return {'x': x, 'W_r': W_r, 'W_k': W_k, 'W_v': W_v, 'mu_r': mu_r, 'mu_k': mu_k}
    _L0_ffn_in = _L0_ffn_setup()
    _L0_c = _w((lambda *s: np.random.randn(*s).astype(np.float32) * 0.05)(1, 256))
    _L0_wmod = _w((lambda *s: np.random.randn(*s).astype(np.float32) * 0.05)(256, 6 * 256) * 256 ** (-0.5))

    def _L1_attn_setup():
        import jax, jax.numpy as jnp
        import numpy as np
        B, S, HID, NH = (4, 1024, 256, 16)
        D = HID // NH
        EPS = 1e-05

        def _delta_scan(q, k, v, beta):
            vsum = v.sum(-1)
            qs = jnp.moveaxis(q, 1, 0)
            ks_ = jnp.moveaxis(k, 1, 0)
            vs = jnp.moveaxis(vsum, 1, 0)
            bs = jnp.moveaxis(beta, 1, 0)

            def step(h, inp):
                q_t, k_t, vsum_t, beta_t = inp
                h = h * beta_t[..., None, None]
                h = h + (k_t * vsum_t[..., None])[:, :, None, :]
                o_t = jnp.einsum('bhj,bhjk->bhk', q_t, h)
                return (h, o_t)
            h0 = jnp.zeros((q.shape[0], q.shape[2], D, D), dtype=q.dtype)
            _, o = jax.lax.scan(step, h0, (qs, ks_, vs, bs))
            return jnp.moveaxis(o, 0, 1)
        key = jax.random.key(seed)
        ks = jax.random.split(key, 8)
        x = jax.random.normal(ks[0], (B, S, HID), dtype=jnp.float32)
        sc = 0.03
        Wq = jax.random.normal(ks[1], (HID, HID), dtype=jnp.float32) * sc
        Wk = jax.random.normal(ks[2], (HID, HID), dtype=jnp.float32) * sc
        Wv = jax.random.normal(ks[3], (HID, HID), dtype=jnp.float32) * sc
        Wbeta = jax.random.normal(ks[4], (HID, NH), dtype=jnp.float32) * sc
        b_beta = jnp.full((NH,), 0.9, dtype=jnp.float32)
        Wo = jax.random.normal(ks[5], (HID, HID), dtype=jnp.float32) * sc
        b_o = jnp.zeros((HID,), dtype=jnp.float32)
        ln_g = jnp.ones((HID,), dtype=jnp.float32)
        ln_b = jnp.zeros((HID,), dtype=jnp.float32)
        return {'x': x, 'Wq': Wq, 'Wk': Wk, 'Wv': Wv, 'Wbeta': Wbeta, 'b_beta': b_beta, 'Wo': Wo, 'b_o': b_o, 'ln_g': ln_g, 'ln_b': ln_b}
    _L1_attn_in = _L1_attn_setup()

    def _L1_ffn_setup():
        import jax, jax.numpy as jnp
        import numpy as np
        B, S, D = (1, 512, 256)
        F = 352
        E = 16
        K = 2
        CAP_FACTOR = 1.25

        def _mlp(h, wg, wu, wd):
            return jax.nn.silu(h @ wg) * (h @ wu) @ wd
        key = jax.random.key(seed)
        ks = jax.random.split(key, 10)
        sd = 0.02
        return {'x': jax.random.normal(ks[0], (B, S, D), jnp.float32), 'router_w': jax.random.normal(ks[1], (D, E), jnp.float32) * sd, 'router_b': jnp.zeros((E,), jnp.float32), 'w_gate': jax.random.normal(ks[2], (E, D, F), jnp.float32) * sd, 'w_up': jax.random.normal(ks[3], (E, D, F), jnp.float32) * sd, 'w_down': jax.random.normal(ks[4], (E, F, D), jnp.float32) * sd, 'sw_gate': jax.random.normal(ks[5], (D, F), jnp.float32) * sd, 'sw_up': jax.random.normal(ks[6], (D, F), jnp.float32) * sd, 'sw_down': jax.random.normal(ks[7], (F, D), jnp.float32) * sd}
    _L1_ffn_in = _L1_ffn_setup()
    _L1_c = _w((lambda *s: np.random.randn(*s).astype(np.float32) * 0.05)(1, 256))
    _L1_wmod = _w((lambda *s: np.random.randn(*s).astype(np.float32) * 0.05)(256, 6 * 256) * 256 ** (-0.5))
    _d = {'L0_attn_x': _L0_attn_in['x'], 'L0_attn_qkv': _L0_attn_in['qkv'], 'L0_attn_wo': _L0_attn_in['wo'], 'L0_ffn_W_r': _L0_ffn_in['W_r'], 'L0_ffn_W_k': _L0_ffn_in['W_k'], 'L0_ffn_W_v': _L0_ffn_in['W_v'], 'L0_ffn_mu_r': _L0_ffn_in['mu_r'], 'L0_ffn_mu_k': _L0_ffn_in['mu_k'], 'L0_c': _L0_c, 'L0_wmod': _L0_wmod, 'L1_attn_Wq': _L1_attn_in['Wq'], 'L1_attn_Wk': _L1_attn_in['Wk'], 'L1_attn_Wv': _L1_attn_in['Wv'], 'L1_attn_Wbeta': _L1_attn_in['Wbeta'], 'L1_attn_b_beta': _L1_attn_in['b_beta'], 'L1_attn_Wo': _L1_attn_in['Wo'], 'L1_attn_b_o': _L1_attn_in['b_o'], 'L1_attn_ln_g': _L1_attn_in['ln_g'], 'L1_attn_ln_b': _L1_attn_in['ln_b'], 'L1_ffn_router_w': _L1_ffn_in['router_w'], 'L1_ffn_router_b': _L1_ffn_in['router_b'], 'L1_ffn_w_gate': _L1_ffn_in['w_gate'], 'L1_ffn_w_up': _L1_ffn_in['w_up'], 'L1_ffn_w_down': _L1_ffn_in['w_down'], 'L1_ffn_sw_gate': _L1_ffn_in['sw_gate'], 'L1_ffn_sw_up': _L1_ffn_in['sw_up'], 'L1_ffn_sw_down': _L1_ffn_in['sw_down'], 'L1_c': _L1_c, 'L1_wmod': _L1_wmod}
    _x0 = _d['L0_attn_x']
    _d['L0_attn_x'] = jax.random.normal(jax.random.fold_in(jax.random.key(seed), 1), (1, 4096, 256), dtype=_x0.dtype)
    del _x0
    return _d

def reference(L0_attn_x, L0_attn_qkv, L0_attn_wo, L0_ffn_W_r, L0_ffn_W_k, L0_ffn_W_v, L0_ffn_mu_r, L0_ffn_mu_k, L0_c, L0_wmod, L1_attn_Wq, L1_attn_Wk, L1_attn_Wv, L1_attn_Wbeta, L1_attn_b_beta, L1_attn_Wo, L1_attn_b_o, L1_attn_ln_g, L1_attn_ln_b, L1_ffn_router_w, L1_ffn_router_b, L1_ffn_w_gate, L1_ffn_w_up, L1_ffn_w_down, L1_ffn_sw_gate, L1_ffn_sw_up, L1_ffn_sw_down, L1_c, L1_wmod):

    def _L0_attn_ref(x, qkv, wo):
        import jax, jax.numpy as jnp
        import numpy as np
        import math
        D_MODEL = 256
        N_HEADS = 16
        DH = D_MODEL // N_HEADS
        THETA = 10000.0

        def _rope_tables(S):
            inv_freq = 1.0 / THETA ** (jnp.arange(0, DH, 2, dtype=jnp.float32) / DH)
            ang = jnp.arange(S, dtype=jnp.float32)[:, None] * inv_freq[None, :]
            cos = jnp.concatenate([jnp.cos(ang), jnp.cos(ang)], axis=-1)
            sin = jnp.concatenate([jnp.sin(ang), jnp.sin(ang)], axis=-1)
            return (cos, sin)

        def _apply_rope(x, cos, sin):
            x1, x2 = jnp.split(x, 2, axis=-1)
            rot = jnp.concatenate([-x2, x1], axis=-1)
            c = cos[None, :, None, :]
            s = sin[None, :, None, :]
            return x * c + rot * s
        B, S, D = x.shape
        QKV = x @ qkv.T
        Q, K, V = jnp.split(QKV, 3, axis=-1)
        q = Q.reshape(B, S, N_HEADS, DH)
        k = K.reshape(B, S, N_HEADS, DH)
        v = V.reshape(B, S, N_HEADS, DH)
        cos, sin = _rope_tables(S)
        q = _apply_rope(q, cos, sin)
        k = _apply_rope(k, cos, sin)
        q = q.transpose(0, 2, 1, 3)
        k = k.transpose(0, 2, 1, 3)
        v = v.transpose(0, 2, 1, 3)
        scores = jnp.einsum('bhsd,bhtd->bhst', q, k) / math.sqrt(float(DH))
        mask = jnp.tril(jnp.ones((S, S), dtype=scores.dtype))
        scores = scores * mask
        scores = jnp.where(scores == 0.0, -jnp.inf, scores)
        attn = jax.nn.softmax(scores, axis=-1)
        out = jnp.einsum('bhst,bhtd->bhsd', attn, v)
        out = out.transpose(0, 2, 1, 3).reshape(B, S, D)
        return out @ wo.T

    def _L0_ffn_ref(x, W_r, W_k, W_v, mu_r, mu_k):
        import jax, jax.numpy as jnp
        import numpy as np
        DIM = 256

        def _reference_tuple_inner(x, W_r, W_k, W_v, mu_r, mu_k):
            B, T, C = x.shape
            x_prev = jnp.concatenate([jnp.zeros((B, 1, C), x.dtype), x[:, :-1, :]], axis=1)
            xr = mu_r * x + (1.0 - mu_r) * x_prev
            xk = mu_k * x + (1.0 - mu_k) * x_prev
            r = jax.nn.sigmoid(jnp.einsum('btc,dc->btd', xr, W_r))
            k = jnp.einsum('btc,dc->btd', xk, W_k)
            k_act = jnp.square(jax.nn.relu(k))
            out = r * jnp.einsum('btc,dc->btd', k_act, W_v)
            new_state = x[:, -1, :]
            return (out, new_state)
        return _reference_tuple_inner(x, W_r, W_k, W_v, mu_r, mu_k)[0]

    def _L1_attn_ref(x, Wq, Wk, Wv, Wbeta, b_beta, Wo, b_o, ln_g, ln_b):
        import jax, jax.numpy as jnp
        import numpy as np
        B, S, HID, NH = (4, 1024, 256, 16)
        D = HID // NH
        EPS = 1e-05

        def _delta_scan(q, k, v, beta):
            vsum = v.sum(-1)
            qs = jnp.moveaxis(q, 1, 0)
            ks_ = jnp.moveaxis(k, 1, 0)
            vs = jnp.moveaxis(vsum, 1, 0)
            bs = jnp.moveaxis(beta, 1, 0)

            def step(h, inp):
                q_t, k_t, vsum_t, beta_t = inp
                h = h * beta_t[..., None, None]
                h = h + (k_t * vsum_t[..., None])[:, :, None, :]
                o_t = jnp.einsum('bhj,bhjk->bhk', q_t, h)
                return (h, o_t)
            h0 = jnp.zeros((q.shape[0], q.shape[2], D, D), dtype=q.dtype)
            _, o = jax.lax.scan(step, h0, (qs, ks_, vs, bs))
            return jnp.moveaxis(o, 0, 1)
        b, s, hid = x.shape
        residual = x
        q = (x @ Wq).reshape(b, s, NH, D)
        k = (x @ Wk).reshape(b, s, NH, D)
        v = (x @ Wv).reshape(b, s, NH, D)
        beta = jax.nn.sigmoid(x @ Wbeta + b_beta)
        o = _delta_scan(q, k, v, beta).reshape(b, s, hid)
        out = o @ Wo + b_o
        y = residual + out
        mu = y.mean(-1, keepdims=True)
        var = ((y - mu) ** 2).mean(-1, keepdims=True)
        return ln_g * (y - mu) * jax.lax.rsqrt(var + EPS) + ln_b

    def _L1_ffn_ref(x, router_w, router_b, w_gate, w_up, w_down, sw_gate, sw_up, sw_down):
        import jax, jax.numpy as jnp
        import numpy as np
        B, S, D = (1, 512, 256)
        F = 352
        E = 16
        K = 2
        CAP_FACTOR = 1.25

        def _mlp(h, wg, wu, wd):
            return jax.nn.silu(h @ wg) * (h @ wu) @ wd
        b, s, d = x.shape
        N = b * s
        NK = N * K
        C = int(np.ceil(CAP_FACTOR * NK / E))
        x_tokens = x.reshape(N, d)
        logits = x_tokens @ router_w + router_b
        probs = jax.nn.softmax(logits, axis=-1)
        vals, idx = jax.lax.top_k(probs, K)
        vals = vals / (jnp.sum(vals, axis=-1, keepdims=True) + 1e-09)
        idx_flat = idx.reshape(NK)
        vals_flat = vals.reshape(NK)
        oh_e = jax.nn.one_hot(idx_flat, E, dtype=x.dtype)
        pos = (jnp.cumsum(oh_e, axis=0) * oh_e).sum(axis=1) - 1
        within = (pos < C).astype(x.dtype)
        pos_c = jnp.clip(pos, 0, C - 1).astype(jnp.int32)
        token_ids = jnp.arange(NK) // K
        x_pair = x_tokens[token_ids] * within[:, None]
        expert_inputs = jnp.zeros((E, C, d), x.dtype).at[idx_flat, pos_c].add(x_pair)
        expert_outputs = jax.vmap(_mlp)(expert_inputs, w_gate, w_up, w_down)
        gathered = expert_outputs[idx_flat, pos_c] * (vals_flat * within)[:, None]
        output_tokens = gathered.reshape(N, K, d).sum(axis=1)
        return x + _mlp(x, sw_gate, sw_up, sw_down) + output_tokens.reshape(b, s, d)
    x = L0_attn_x
    mod = (_silu(L0_c) @ L0_wmod).reshape(L0_c.shape[0], 6, 1, -1)
    sa, ca, ga, sb, cb, gb = (mod[:, 0], mod[:, 1], mod[:, 2], mod[:, 3], mod[:, 4], mod[:, 5])
    ga = (2 * (ga >= 0) - 1) * jnp.maximum(jnp.abs(ga), 0.25)
    gb = (2 * (gb >= 0) - 1) * jnp.maximum(jnp.abs(gb), 0.25)
    h = _layernorm(x, axis=-1) * (1 + ca) + sa
    x = x + ga * _L0_attn_ref(h, L0_attn_qkv, L0_attn_wo)
    h = _layernorm(x, axis=-1) * (1 + cb) + sb
    x = x + gb * _L0_ffn_ref(h, L0_ffn_W_r, L0_ffn_W_k, L0_ffn_W_v, L0_ffn_mu_r, L0_ffn_mu_k)
    mod = (_silu(L1_c) @ L1_wmod).reshape(L1_c.shape[0], 6, 1, -1)
    sa, ca, ga, sb, cb, gb = (mod[:, 0], mod[:, 1], mod[:, 2], mod[:, 3], mod[:, 4], mod[:, 5])
    ga = (2 * (ga >= 0) - 1) * jnp.maximum(jnp.abs(ga), 0.25)
    gb = (2 * (gb >= 0) - 1) * jnp.maximum(jnp.abs(gb), 0.25)
    h = _layernorm(x, axis=-1) * (1 + ca) + sa
    x = x + ga * _L1_attn_ref(h, L1_attn_Wq, L1_attn_Wk, L1_attn_Wv, L1_attn_Wbeta, L1_attn_b_beta, L1_attn_Wo, L1_attn_b_o, L1_attn_ln_g, L1_attn_ln_b)
    h = _layernorm(x, axis=-1) * (1 + cb) + sb
    x = x + gb * _L1_ffn_ref(h, L1_ffn_router_w, L1_ffn_router_b, L1_ffn_w_gate, L1_ffn_w_up, L1_ffn_w_down, L1_ffn_sw_gate, L1_ffn_sw_up, L1_ffn_sw_down)
    return x

_drawn_inputs = setup_inputs


def setup_inputs(seed=0):
    import zlib

    import numpy as np

    out = dict(_drawn_inputs(seed))
    spreads = {'L1_attn_b_beta': (0.8999999761581421, 0.6),
     'L1_attn_b_o': (0.0, 0.499),
     'L1_attn_ln_g': (1.0, 0.2),
     'L1_attn_ln_b': (0.0, 0.347),
     'L1_ffn_router_b': (0.0, 0.8)}
    factors = {'L0_attn_qkv': 8.0,
     'L0_attn_wo': 8.0,
     'L0_ffn_W_r': 8.0,
     'L0_ffn_W_k': 2.903,
     'L0_ffn_mu_r': 8.0,
     'L0_ffn_mu_k': 4.823,
     'L0_c': 2.75,
     'L0_wmod': 2.681,
     'L1_ffn_router_w': 8.0,
     'L1_ffn_w_gate': 8.0,
     'L1_ffn_w_up': 8.0,
     'L1_ffn_w_down': 8.0,
     'L1_ffn_sw_gate': 8.0,
     'L1_ffn_sw_up': 8.0,
     'L1_ffn_sw_down': 8.0}
    for name, (base, spread) in spreads.items():
        noise = np.random.default_rng([zlib.crc32(name.encode()), seed]).standard_normal(out[name].shape)
        drawn = base * np.exp(spread * noise) if base else spread * noise
        out[name] = jnp.asarray(drawn.astype(out[name].dtype))
    for name, factor in factors.items():
        out[name] = (out[name] * factor).astype(out[name].dtype)
    return out
```

```python
from contextlib import ExitStack

import concourse.bass as bass
import numpy as np
from concourse import mybir

ALU = mybir.AluOpType
ACT = mybir.ActivationFunctionType
AX = mybir.AxisListType
BF16 = mybir.dt.bfloat16
F32 = mybir.dt.float32
U32 = mybir.dt.uint32

P = 128
T = 4096
D = 256
KC = D // P
NH = 16
DH = D // NH
BT = 512
NB = T // BT
TT = BT // P
NT = T // P
HG = 4
NG = NH // HG
EPS = 1e-5
FF = 352
FM = [(0, P), (P, P), (2 * P, FF - 2 * P)]
E_ = 16
CAP = 640
CT = CAP // P
SCORE_LIMIT = 70.0
BIG = 3e38

Q_PART = [0, 0, 0, 1, 1, 1, 2, 2]
K_PART = [0, 1, 2, 0, 1, 2, 0, 1]


def pipeline(eng, stages, blocks=NB):
    top = max(skew for skew, _ in stages)
    start = top + top % 2

    def step(t, i=None):
        for skew, stage in stages:
            b = t - skew
            if i is not None:
                stage(b + 2 * i, b % 2, b // 2 + i)
            elif 0 <= b < blocks:
                stage(b, b % 2, b // 2)

    for t in range(start):
        step(t)
    pairs = (blocks - start) // 2
    if pairs:
        with eng.Fori(0, pairs) as i:
            step(start, i)
            step(start + 1, i)
    for t in range(start + 2 * pairs, blocks + top):
        step(t)


def off_diagonal(j):
    first = min(2, TT * j)
    return first, (TT * j - first) // 3, (TT * j - first) % 3


def steps_until(j):
    return 2 * (j + 1) * (j + 2) if j >= 0 else 0


class Step:

    def __init__(self, g, j, kt, static_kt, loop_kt=None):
        self.g, self.j, self.kt = g, j, kt
        self.first = static_kt == 0 and loop_kt is None
        self.second = static_kt == 1 and loop_kt is None
        self.n0 = 2 * j * (j + 1)
        self.slot = (self.n0 + static_kt) % 3
        d = static_kt - TT * j if loop_kt is None else -1
        self.diag = d if d >= 0 else None
        self.last = self.diag == TT - 1
        self.w0 = P * d if d > 0 else 0
        self.count = g * STEPS + self.n0 + kt

STEPS = sum(TT * (j + 1) for j in range(NB))


def walk(eng, emit):
    with eng.Fori(0, NG) as g:
        for j in range(NB):
            first, threes, rest = off_diagonal(j)
            for k in range(first):
                emit(Step(g, j, k, k))
            if threes:
                with eng.Fori(0, threes) as i:
                    for m in range(3):
                        emit(Step(g, j, first + 3 * i + m, first + m, i))
            for k in range(first + 3 * threes, TT * (j + 1)):
                emit(Step(g, j, k, k))


class Store:
    pass


def allocate(nc, ctx, ins, out):
    m = Store()
    m.ins, m.out = ins, out

    def sb(name, shape, dt=F32):
        return ctx.enter_context(nc.sbuf_tensor(name, shape, dt))

    def scratch(name, shape, dt=F32):
        return nc.dram_tensor(name, shape, dt, kind="Internal").ap()

    m.sb = sb
    m.ident = sb("ident", [P, P])
    m.mod_cols = sb("mod_cols", [P, 2, 4, KC])
    m.gates = sb("gates", [P, 2, 2, D])
    m.mod_rows = sb("mod_rows", [P, 4, D])
    m.reach = sb("reach", [P, 1])
    m.bounded = sb("bounded", [P, 1], U32)
    m.values = sb("values", [P, NT, D])
    m.mhalf = sb("mhalf", [P, TT])
    m.arena = sb("arena", [P, 32768])
    m.arena2 = sb("arena2", [P, 9728])
    m.parts = scratch("parts_dram", [2, 3, D, T], BF16)
    m.attn = scratch("attn_dram", [T, D])
    m.k_stack = m.arena[:, :].bitcast(BF16).rearrange("p (h t) -> p h t", h=NH)
    m.pool_chain = ctx.enter_context(nc.semaphore("pool_chain"))
    m.scatter_at = sb("scatter_at", [P, 2, NT], U32)
    m.gather_at = sb("gather_at", [P, 2, NT], U32)
    m.slots_in = scratch("slots_in_dram", [E_ * CAP, D])
    m.slots_out = scratch("slots_out_dram", [E_ * CAP, D])
    m.held = ctx.enter_context(nc.semaphore("held"))
    m.weights_in = ctx.enter_context(nc.semaphore("weights_in"))
    m.qkv_in = ctx.enter_context(nc.semaphore("qkv_in"))
    a = Carver(m.arena, HG * T // 2)
    m.w_qkv, m.w_rot = a.take(KC, 3 * D), a.take(KC, 2 * D)
    m.project_at = a.at
    m.zeroed = ctx.enter_context(nc.semaphore("zeroed"))
    place_weights(m)
    m.kload_first = ctx.enter_context(nc.semaphore("kload_first"))
    m.kload_last = ctx.enter_context(nc.semaphore("kload_last"))
    m.stored = [ctx.enter_context(nc.semaphore(f"stored{w}")) for w in range(4)]
    return m


class Carver:

    def __init__(self, tensor, at=0):
        self.tensor, self.at = tensor, at
        self.size = tensor.shape[1]

    def take(self, *shape, dt=F32):
        words = int(np.prod(shape)) * (2 if dt == BF16 else 4) // 4
        view = self.tensor[:, self.at:self.at + words]
        self.at += words
        assert self.at <= self.size, (self.at, self.size)
        if dt != F32:
            view = view.bitcast(dt)
        if len(shape) > 1:
            names = " ".join(f"a{i}" for i in range(len(shape)))
            view = view.rearrange(f"p ({names}) -> p {names}", **{f"a{i}": s for i, s in enumerate(shape)})
        return view


def place_weights(m):
    a = Carver(m.arena)
    (m.w_o, m.w_r, m.w_k, m.w_v, m.l1_k, m.l1_q, m.l1_v, m.l1_beta, m.l1_o) = (a.take(KC, D) for _ in range(9))
    m.router = a.take(KC, E_)
    m.s_gate, m.s_up = a.take(KC, FF), a.take(KC, FF)
    m.s_down = a.take(len(FM), D)
    m.mu = a.take(2, KC)
    m.b_beta = a.take(KC)
    m.ln_gain, m.ln_shift, m.b_o = a.take(D), a.take(D), a.take(D)
    m.router_b = a.take(E_)
    m.beta_narrow = a.take(KC, NH)
    m.logits = a.take(NT, E_)
    m.h_even = a.take(KC, T + 1)
    m.odd_at = a.at
    m.h_odd = a.take(KC, T)
    m.h_rows = a.take(NT, D)
    m.x = m.values


def load_weights(m, eng):
    count = 0

    def load(dst, src, **kw):
        nonlocal count
        eng.dma_start(dst, src, **kw).then_inc(m.weights_in, 16)
        count += 1

    for dst, name in ((m.w_o, "woT"), (m.w_r, "W_rT"), (m.w_k, "W_kT"), (m.w_v, "W_vT"), (m.l1_k, "L1_attn_Wk"),
                      (m.l1_q, "L1_attn_Wq"), (m.l1_v, "L1_attn_Wv"), (m.beta_narrow, "L1_attn_Wbeta"), (m.l1_o, "L1_attn_Wo"),
                      (m.router, "L1_ffn_router_w"), (m.s_gate, "L1_ffn_sw_gate"), (m.s_up, "L1_ffn_sw_up")):
        load(dst, m.ins[name].rearrange("(k p) n -> p k n", p=P))
    load(m.s_down[:, 0:2], m.ins["L1_ffn_sw_down"][0:2 * P].rearrange("(k p) n -> p k n", p=P))
    load(m.s_down[0:FF - 2 * P, 2], m.ins["L1_ffn_sw_down"][2 * P:FF])
    for k, name in enumerate(("L0_ffn_mu_r", "L0_ffn_mu_k")):
        load(m.mu[:, k], m.ins[name].rearrange("(k p) -> p k", p=P), allow_slow_non_contiguous=True)
    load(m.b_beta, m.ins["b_beta_rep"].rearrange("(k p) -> p k", p=P), allow_slow_non_contiguous=True)
    for dst, name in ((m.ln_gain, "L1_attn_ln_g"), (m.ln_shift, "L1_attn_ln_b"), (m.b_o, "L1_attn_b_o"),
                      (m.router_b, "L1_ffn_router_b")):
        load(dst, m.ins[name].rearrange("(a n) -> a n", a=1).to_broadcast([P, m.ins[name].shape[0]]))
    m.weights_expected = 16 * count


def phase_modulation(nc, m):
    with ExitStack() as ctx:
        def sem(name):
            return ctx.enter_context(nc.semaphore(name))

        a = Carver(m.arena)
        wmod = a.take(2, KC, 6 * D)
        c_cols = a.take(2, KC)
        t0 = a.take(2, KC)
        t1 = a.take(2, KC)
        t2 = a.take(2, KC)
        silu = a.take(2, KC)
        silu_wide = a.take(2, KC, P)
        ones = a.take(P)
        assert a.at <= HG * T // 2
        ps_rows = ctx.enter_context(nc.psum_tensor("ps_rows", [P, 4, 512], F32))
        ps_rows1 = ctx.enter_context(nc.psum_tensor("ps_rows1", [P, 2, 2, D], F32))
        ps_cols = ctx.enter_context(nc.psum_tensor("ps_cols", [P, 512], F32))
        loaded, exped, silued, rows_done, cols_done, chain, wide = map(
            sem, ["mod_loaded", "mod_exped", "mod_silued", "mod_rows", "mod_cols_s", "mod_chain", "mod_wide"])
        block = ctx.enter_context(nc.Block())

        @block.sync
        def _(sp):
            for la, name in enumerate(("L0", "L1")):
                with nc.allow_non_contiguous_dma(reason="256 words of c onto partitions"):
                    sp.dma_start(c_cols[:, la, :], m.ins[name + "_c"].rearrange("a (k p) -> p (a k)", p=P)).then_inc(loaded, 16)
                sp.dma_start(wmod[:, la, :, :], m.ins[name + "_wmod"].rearrange("(k p) n -> p k n", p=P)).then_inc(loaded, 16)
            sp.dma_start(m.ident[:], m.ins["ident"]).then_inc(loaded, 16)
            for dst, name in ((m.w_qkv, "qkvT"), (m.w_rot, "qk_swapT")):
                sp.dma_start(dst, m.ins[name].rearrange("(k p) n -> p k n", p=P)).then_inc(m.qkv_in, 16)

        @block.scalar
        def _(act):
            act.wait_ge(loaded, 80)
            act.activation(t0, c_cols, ACT.Exp, scale=-1.0).then_inc(exped, 1)

        @block.vector
        def _(dve):
            steps = [0]

            def link(ins):
                steps[0] += 1
                ins.then_inc(chain, 1)
                dve.wait_ge(chain, steps[0])

            dve.memset(ones, 1.0)
            dve.wait_ge(exped, 1)
            link(dve.tensor_scalar(t1, t0, 1.0, None, ALU.add))
            link(dve.reciprocal(t2, t1))
            link(dve.tensor_tensor(silu, c_cols, t2, ALU.mult))
            for la in range(2):
                for k in range(KC):
                    last = dve.tensor_scalar(silu_wide[:, la, k, :], ones, silu[:, la, k:k + 1], None, ALU.mult)
            last.then_inc(silued, 1)
            dve.wait_ge(cols_done, 1)
            cols = ps_cols[:, 0:16].rearrange("p (l q k) -> p l q k", l=2, q=4)
            link(dve.tensor_copy(m.mod_cols[:], cols))
            for la in range(2):
                for q in (1, 3):
                    link(dve.tensor_scalar(m.mod_cols[:, la, q, :], m.mod_cols[:, la, q, :], 1.0, None, ALU.add))
            dve.wait_ge(rows_done, 1)
            dve.tensor_copy(m.mod_rows[:], ps_rows1[:].rearrange("p a b n -> p (a b) n"))
            dve.tensor_copy(m.gates[:], ps_rows[:, :, 0:D].rearrange("p (l g) n -> p l g n", l=2))

        @block.tensor
        def _(pe):
            pe.wait_ge(loaded, 80)
            pe.wait_ge(silued, 1)
            for la in range(2):
                for q, at in enumerate((0, 1, 3, 4)):
                    for mm in range(KC):
                        c = (la * 4 + q) * KC + mm
                        for k in range(KC):
                            last = pe.matmul(ps_cols[:, c:c + 1], wmod[:, la, k, at * D + mm * P:at * D + mm * P + P],
                                             silu[:, la, k:k + 1], start=k == 0, stop=k == KC - 1)
            last.then_inc(cols_done, 1)
            for la in range(2):
                for g, at in enumerate((2, 5)):
                    for k in range(KC):
                        last = pe.matmul(ps_rows[:, 2 * la + g, 0:D], silu_wide[:, la, k, :],
                                         wmod[:, la, k, at * D:at * D + D], start=k == 0, stop=k == KC - 1)
            for q, at in enumerate((0, 1, 3, 4)):
                for k in range(KC):
                    last = pe.matmul(ps_rows1[:, q // 2, q % 2, :], silu_wide[:, 1, k, :],
                                     wmod[:, 1, k, at * D:at * D + D], start=k == 0, stop=k == KC - 1)
            last.then_inc(rows_done, 1)


def hold(m, eng, sem, value):
    eng.wait_ge(sem, value)
    eng.sem_inc(m.held, 1)


def pick(view, i):
    if isinstance(i, int):
        return view[:, i]
    rest = " ".join(f"z{n}" for n in range(len(view.shape) - 2))
    first, others = rest.split(" ")[0], " ".join(rest.split(" ")[1:])
    return view[:, bass.ds(i, 1)].rearrange(f"p a {rest} -> p (a {first}) {others}")


def clear_slots(m, eng):
    fill = m.slots_in.rearrange("(c r) n -> c r n", r=m.ins["zeros"].shape[0])
    for c in range(fill.shape[0]):
        eng.dma_start(fill[c], m.ins["zeros"]).then_inc(m.zeroed, 16)
    m.zeroed_expected = 16 * fill.shape[0]


def load_first_k(m, eng, b, sem):
    for r in range(8):
        eng.dma_start(m.k_stack[DH * r:DH * r + DH, 0:HG, bass.ds(b * BT, BT)],
                      m.parts[1, K_PART[r], 0:HG * DH, bass.ds(b * BT, BT)].rearrange("(h d) n -> d h n", d=DH)).then_inc(sem, 16)


def wait_parts_stored(m, eng):
    for w in range(4):
        eng.wait_ge(m.stored[w], 16 * (NB + 1))


def phase_project(nc, m):
    with ExitStack() as ctx:
        own = []

        def sem(name):
            own.append(nc.alloc_semaphore(name="a_" + name))
            return own[-1]

        def pb(name, shape):
            return ctx.enter_context(nc.psum_tensor(name, shape, F32))

        a = Carver(m.arena, m.project_at)
        tables = a.take(2, 2, BT)
        x = a.take(2, TT, D)
        xn = a.take(2, TT, D)
        hT = a.take(2, KC, BT)
        w_qkv, w_rot = m.w_qkv, m.w_rot
        rolled = a.take(2, 2, BT)
        rot = a.take(4, BT)
        rest = a.take(4, BT)
        parts = a.take(4, 3, BT, dt=BF16)
        sq = a.take(4, BT, dt=BF16)
        sign = a.take(2, 2, D)
        size = a.take(2, 2, D)
        a = Carver(m.arena2)
        stats = a.take(2, TT, 6)
        mv = a.take(2, TT, 2)
        ve = a.take(2, TT)
        rstd = a.take(2, TT)
        mhalf = a.take(TT)
        norms = a.take(2, 2, NT)
        k_so_far = a.take(2, NT)
        reach = a.take(2, NT)
        widest = a.take(1)
        bones_f = a.take(P)
        bones = a.take(P, dt=BF16)

        ps_t = pb("ps_t", [P, KC, BT])
        ps_p = pb("ps_p", [P, 2, 2, BT])
        ps_v = pb("ps_v", [P, 2 * D])
        ps_n = pb("ps_n", [P, BT])

        x_in = [sem("x_in0"), sem("x_in1")]
        tab_in = [sem("tab_in0"), sem("tab_in1")]
        w_in, st, mvs, rst, xns = sem("w_in"), sem("stats"), sem("mv"), sem("rstd"), sem("xn")
        tr, hts, proj, rolls, rots = sem("transposed"), sem("hT"), sem("proj"), sem("rolled"), sem("rot")
        sqs, rests, p2s, p3s = sem("sq"), sem("rest"), sem("p2"), sem("p3")
        vs, vevac, nrm, nused = sem("v"), sem("v_evacuated"), sem("norm"), sem("norm_used")
        consts, tail, gate_chain = sem("consts"), sem("tail"), sem("gate_chain")
        stored = m.stored
        x_dram = m.ins["L0_attn_x"].rearrange("a (b t p) d -> p (a b) t d", p=P, t=TT)
        tab_dram = m.ins["rope"].rearrange("c p (b n) -> p b c n", n=BT)
        block = ctx.enter_context(nc.Block())

        @block.sync
        def _(sp):
            for w in range(4):
                sp.sem_inc(stored[w], 16)
            sp.dma_start(bones_f, m.ins["head_ones"]).then_inc(w_in, 16)

            def load_x(b, s, h):
                hold(m, sp, xns, b + 1)
                sp.dma_start(x[:, s], pick(x_dram, b)).then_inc(x_in[s], 16)

            def load_tables(b, s, h):
                hold(m, sp, rots, 4 * b + 4)
                sp.dma_start(tables[:, s], pick(tab_dram, b)).then_inc(tab_in[s], 16)

            def store(b, s, h):
                for w in range(4):
                    hold(m, sp, p3s, 4 * b + w + 1)
                    sp.dma_start(m.parts[w // 2, :, (w % 2) * P:(w % 2) * P + P, bass.ds(b * BT, BT)].rearrange("c p n -> p c n"),
                                 parts[:, w]).then_inc(stored[w], 16)

            def load_k(b, s, h):
                if isinstance(b, int) and b == NB - 1:
                    return
                hold(m, sp, stored[2], 16 * (b + 2))
                load_first_k(m, sp, b, m.kload_first)

            pipeline(sp, [(0, load_x), (1, load_tables), (3, store), (4, load_k)])

        @block.vector
        def _(dve):
            dve.sem_inc(xns, 2)
            dve.sem_inc(rolls, 2)
            dve.sem_inc(rots, 8)
            dve.sem_inc(nused, 1)
            dve.wait_ge(w_in, 16)
            dve.tensor_copy(bones, bones_f).then_inc(consts, 1)

            def statistics(b, s, h):
                dve.wait_ge(x_in[s], 16 * (h + 1))
                for t in range(TT):
                    last = dve.bn_stats(stats[:, s, t], x[:, s, t])
                last.then_inc(st, 1)
                hold(m, dve, st, b + 1)
                for t in range(TT):
                    last = dve.bn_aggr(mv[:, s, t], stats[:, s, t])
                last.then_inc(mvs, 1)

            def normalise(b, s, h):
                dve.wait_ge(rst, b + 1)
                dve.wait_ge(tr, b + 1)
                for t in range(TT):
                    last = dve.tensor_scalar(xn[:, s, t], x[:, s, t], mv[:, s, t, 0:1], rstd[:, s, t:t + 1],
                                             ALU.subtract, ALU.mult)
                last.then_inc(xns, 1)

            def finish_modulation(b, s, h):
                if not (isinstance(b, int) and b == 0):
                    return
                steps = [0]

                def link(ins):
                    steps[0] += 1
                    ins.then_inc(gate_chain, 1)
                    dve.wait_ge(gate_chain, steps[0])

                for q in (1, 3):
                    dve.tensor_scalar(m.mod_rows[:, q, :], m.mod_rows[:, q, :], 1.0, None, ALU.add)
                dve.tensor_scalar(size, m.gates[:], -1.0, None, ALU.mult)
                link(dve.tensor_scalar(sign, m.gates[:], 0.0, 2.0, ALU.is_ge, ALU.mult))
                dve.tensor_scalar(sign, sign, -1.0, None, ALU.add)
                link(dve.tensor_tensor(size, size, m.gates[:], ALU.max))
                link(dve.tensor_scalar(size, size, 0.25, None, ALU.max))
                dve.tensor_tensor(m.gates[:], size, sign, ALU.mult)

            def roll(w):
                def stage(b, s, h):
                    g = 4 * b + w
                    if w == 0:
                        dve.wait_ge(tab_in[s], 16 * (h + 1))
                    dve.wait_ge(proj, g + 1)
                    dve.tensor_tensor(rolled[:, w % 2, 0], ps_p[:, w % 2, 0], tables[:, s, 0], ALU.mult)
                    dve.tensor_tensor(rolled[:, w % 2, 1], ps_p[:, w % 2, 1], tables[:, s, 1], ALU.mult).then_inc(rolls, 1)
                return stage

            def rotate(w):
                def stage(b, s, h):
                    g = 4 * b + w
                    dve.wait_ge(rolls, g + 3)
                    dve.wait_ge(rests, g + 1)
                    dve.tensor_tensor(rot[:, w], rolled[:, w % 2, 0], rolled[:, w % 2, 1], ALU.add).then_inc(rots, 1)
                return stage

            def take_norm(w):
                def stage(b, s, h):
                    dve.wait_ge(nrm, 4 * b + w + 5)
                    dve.tensor_reduce(norms[:, w // 2, w % 2, bass.ds(TT * b, TT)], ps_n[:, :].rearrange("p (t n) -> p t n", t=TT),
                                      AX.X, ALU.max).then_inc(nused, 1)
                return stage

            pipeline(dve, [(0, statistics)] + [one for w in range(4) for one in ((2, roll(w)), (3, take_norm(w)), (2, rotate(w)))]
                     + [(0, normalise), (1, finish_modulation)])
            dve.wait_ge(nused, 4 * NB + 1)
            for half in range(2):
                last = dve.tensor_tensor_scan(k_so_far[:, half], norms[:, 1, half], norms[:, 1, half], 0.0, ALU.max, ALU.max)
            last.then_inc(tail, 1)
            dve.wait_ge(tail, 1)
            dve.tensor_tensor(reach, norms[:, 0], k_so_far, ALU.mult).then_inc(tail, 1)
            dve.wait_ge(tail, 2)
            dve.tensor_reduce(widest, reach, AX.XY, ALU.max).then_inc(tail, 1)
            dve.wait_ge(tail, 4)
            dve.tensor_reduce(m.reach[0:1], ps_n[0:1, 0:P], AX.X, ALU.max).then_inc(tail, 1)
            dve.wait_ge(tail, 5)
            dve.tensor_scalar(widest[0:1], m.reach[0:1], (SCORE_LIMIT * DH ** 0.5) ** 2 / 1.02, None, ALU.is_le).then_inc(tail, 1)
            dve.wait_ge(tail, 6)
            dve.tensor_copy(m.bounded[0:1], widest[0:1])

        @block.gpsimd
        def _(pool):
            pool.sem_inc(rests, 4)
            pool.memset(mhalf, -0.5).then_inc(consts, 1)
            pool.wait_ge(consts, 2)

            def inverse_deviation(b, s, h):
                hold(m, pool, mvs, b + 1)
                pool.tensor_scalar(ve[:, s], mv[:, s, :, 1], EPS, None, ALU.add).then_inc(m.pool_chain, 1)
                hold(m, pool, m.pool_chain, b + 1)
                pool.tensor_tensor(rstd[:, s], ve[:, s], mhalf, ALU.pow).then_inc(rst, 1)

            def split(b, s, h):
                def second(w):
                    hold(m, pool, sqs, 4 * b + w + 1)
                    pool.tensor_tensor(rest[:, w], rot[:, w], parts[:, w, 0], ALU.subtract).then_inc(rests, 1)

                def third(w):
                    hold(m, pool, p2s, 4 * b + w + 1)
                    pool.tensor_tensor(parts[:, w, 2], rest[:, w], parts[:, w, 1], ALU.subtract).then_inc(p3s, 1)

                second(0)
                for w in range(1, 4):
                    second(w)
                    third(w - 1)
                third(3)

            pipeline(pool, [(0, inverse_deviation), (2, split)])

        @block.scalar
        def _(act):
            act.sem_inc(hts, 1)
            act.sem_inc(vevac, 1)

            def modulate(b, s, h):
                act.wait_ge(tr, b + 3)
                act.wait_ge(vs, 2 * b + 2)
                for k in range(KC):
                    last = act.activation(hT[:, s, k], ps_t[:, k], ACT.Identity, bias=m.mod_cols[:, 0, 0, k:k + 1],
                                          scale=m.mod_cols[:, 0, 1, k:k + 1])
                last.then_inc(hts, 1)

            def first(w):
                def stage(b, s, h):
                    act.wait_ge(rots, 4 * b + w + 9)
                    act.wait_ge(stored[w], 16 * (b + 1))
                    act.activation(parts[:, w, 0], rot[:, w], ACT.Copy)
                    act.wait_ge(nrm, 4 * b + w + 1)
                    act.activation(sq[:, w], rot[:, w], ACT.Square).then_inc(sqs, 1)
                return stage

            def second(w):
                def stage(b, s, h):
                    act.wait_ge(rests, 4 * b + w + 5)
                    act.activation(parts[:, w, 1], rest[:, w], ACT.Copy).then_inc(p2s, 1)
                return stage

            def keep_v(c):
                def stage(b, s, h):
                    act.wait_ge(vs, 2 * b + c + 5)
                    act.activation(m.values[:, bass.ds(TT * b + 2 * c, 2), :].rearrange("p t n -> p (t n)"), ps_v[:, :],
                                   ACT.Copy).then_inc(vevac, 1)
                return stage

            pipeline(act, [(2, first(0)), (2, first(1)), (2, second(0)), (1, modulate), (2, first(2)), (2, second(1)),
                           (2, first(3)), (2, second(2)), (2, keep_v(0)), (2, keep_v(1)), (2, second(3))])

        @block.tensor
        def _(pe):
            pe.sem_inc(tr, 2)
            pe.sem_inc(vs, 4)
            pe.sem_inc(nrm, 4)
            pe.wait_ge(m.qkv_in, 32)
            pe.wait_ge(consts, 1)

            def transposes(b, s, h):
                pe.wait_ge(xns, b + 3)
                pe.wait_ge(hts, b + 1)
                for k in range(KC):
                    for t in range(TT):
                        last = pe.transpose(ps_t[:, k, t * P:t * P + P], xn[:, s, t, k * P:k * P + P], m.ident[:])
                last.then_inc(tr, 1)

            def project(w):
                def stage(b, s, h):
                    pe.wait_ge(hts, b + 2)
                    pe.wait_ge(rolls, 4 * b + w + 1)
                    for r, wt in enumerate((w_qkv, w_rot)):
                        for k in range(KC):
                            last = pe.matmul(ps_p[:, w % 2, r], wt[:, k, w * P:w * P + P], hT[:, s, k], start=k == 0, stop=k == KC - 1)
                    last.then_inc(proj, 1)
                return stage

            def value(c):
                def stage(b, s, h):
                    pe.wait_ge(vevac, 2 * b + c + 1)
                    for t in range(2):
                        for k in range(KC):
                            at = (2 * c + t) * P
                            last = pe.matmul(ps_v[:, t * D:t * D + D], hT[:, s, k, at:at + P], w_qkv[:, k, 2 * D:3 * D],
                                             start=k == 0, stop=k == KC - 1)
                    last.then_inc(vs, 1)
                return stage

            def norm(w):
                def stage(b, s, h):
                    pe.wait_ge(sqs, 4 * b + w + 1)
                    pe.wait_ge(nused, 4 * b + w + 1)
                    pe.matmul(ps_n[:, :], bones, sq[:, w], start=True, stop=True).then_inc(nrm, 1)
                return stage

            pipeline(pe, [(2, project(0)), (3, norm(0)), (2, project(1)), (3, norm(1)), (1, transposes), (2, project(2)),
                          (3, norm(2)), (2, value(0)), (2, project(3)), (3, norm(3)), (2, value(1))])
            pe.wait_ge(tail, 3)
            pe.transpose(ps_n[0:1, 0:P], widest, m.ident[:]).then_inc(tail, 1)

    nc.clear_and_free_semaphores(own)
    nc.all_engine_barrier()


def phase_attend(nc, m):
    with ExitStack() as ctx:
        own = []

        def sem(name):
            own.append(nc.alloc_semaphore(name="b_" + name))
            return own[-1]

        def pb(name, shape):
            return ctx.enter_context(nc.psum_tensor(name, shape, F32))

        a = Carver(m.arena2)
        q_stack = a.take(2, HG, BT, dt=BF16)
        probs = a.take(3, HG, BT)
        v_pad = a.take(3, HG, 32)
        o_raw = a.take(BT)
        recips = a.take(TT, HG)
        o_out = a.take(2, TT, HG, DH)

        ps_s = pb("ps_s", [P, 3, 2, BT])
        ps_o = pb("ps_o", [P, 2, BT])

        scored, exped, bank, probs_free, v_in = sem("scored"), sem("exped"), sem("bank_free"), sem("probs_free"), sem("v_in")
        masked, kload, o_copied = sem("masked"), sem("k_loaded"), sem("o_copied")
        o_turned, o_ready, o_done, consts = sem("o_turned"), sem("o_ready"), sem("o_done"), sem("consts")
        recip_done = sem("recip_done")
        q_in = [sem("q_in0"), sem("q_in1")]
        o_stored = [sem("o_stored0"), sem("o_stored1")]
        block = ctx.enter_context(nc.Block())

        def next_group(g):
            return nc.s_assert_within(g + 1, 1, NG - 1,
                                      skip_runtime_bounds_check_because="the branch is taken below the last group only")

        def bounded(eng):
            return eng.value_load(m.bounded[0:1, 0:1], min_val=0, max_val=1)

        @block.sync
        def _(sp):
            for s in range(2):
                sp.sem_inc(o_stored[s], 16)
            sp.sem_inc(kload, 128)

            def store(g, j):
                hold(m, sp, o_ready, g * NB + j + 3)
                with nc.allow_non_contiguous_dma(reason="256 byte runs"):
                    for t in range(TT):
                        sp.dma_start(m.attn[j * BT + t * P:j * BT + t * P + P, bass.ds(g * HG * DH, HG * DH)],
                                     o_out[:, j % 2, t].rearrange("p h d -> p (h d)")).then_inc(o_stored[j % 2], 16)

            def load_q(g, j, before):
                hold(m, sp, scored, 2 * before + 1)
                for r in range(8):
                    sp.dma_start(q_stack[DH * r:DH * r + DH, j % 2],
                                 m.parts[0, Q_PART[r], bass.ds(g * HG * DH, HG * DH), j * BT:j * BT + BT]
                                 .rearrange("(h d) n -> d h n", d=DH)).then_inc(q_in[j % 2], 16)

            with sp.If(bounded(sp) > 0):
                for w in range(2):
                    sp.wait_ge(m.stored[w], 16 * 2)
                load_q(0, 0, 0)
                wait_parts_stored(m, sp)
                load_first_k(m, sp, NB - 1, m.kload_last)
                with sp.Fori(0, NG) as g:
                    for j in range(NB):
                        if j > 0:
                            load_q(g, j, g * STEPS + steps_until(j - 2))
                        if j >= 2:
                            store(g, j - 2)
                        if j == 2:
                            with sp.If(g < NG - 1):
                                g1 = next_group(g)
                                for r in range(8):
                                    sp.dma_start(m.k_stack[DH * r:DH * r + DH, bass.ds(g1 * HG, HG), :],
                                                 m.parts[1, K_PART[r], bass.ds(g1 * HG * DH, HG * DH), :]
                                                 .rearrange("(h d) n -> d h n", d=DH)).then_inc(kload, 16)
                        if j == 2:
                            with sp.If(g > NG - 2):
                                load_weights(m, sp)
                        if j == 5:
                            with sp.If(g > NG - 2):
                                clear_slots(m, sp)
                    with sp.If(g < NG - 1):
                        load_q(next_group(g), 0, g * STEPS + steps_until(NB - 2))
                    store(g, NB - 2)
                    store(g, NB - 1)
                for s in range(2):
                    sp.wait_ge(o_stored[s], 16 + 64 * NG * NB // 2)

        @block.tensor
        def _(pe):
            pe.sem_inc(probs_free, 3)
            pe.sem_inc(scored, 1)
            pe.wait_ge(consts, 1)
            pe.wait_ge(m.kload_first, 16 * 8 * (NB - 1))

            def score(step, pair):
                u = 2 * step.count + pair
                if step.first and pair == 0:
                    pe.wait_ge(q_in[step.j % 2], 128 * (step.g * NB // 2 + step.j // 2 + 1))
                    if step.j == 0:
                        pe.wait_ge(kload, 128 * (step.g + 1))
                    if step.j == NB - 1:
                        pe.wait_ge(m.kload_last, 128)
                pe.wait_ge(bank, u + 1)
                for h in range(2):
                    head = step.g * HG + 2 * pair + h
                    last = pe.matmul(ps_s[:, (2 * step.slot + pair) % 3, h, step.w0:],
                                     m.k_stack[:, bass.ds(head, 1), bass.ds(step.kt * P, P)].rearrange("p a n -> p (a n)"),
                                     q_stack[:, step.j % 2, 2 * pair + h, step.w0:], start=True, stop=True)
                last.then_inc(scored, 1)

            def weigh(step):
                n = step.count
                if step.first:
                    pe.wait_ge(o_ready, step.g * NB + step.j + 1)
                pe.wait_ge(v_in, n + 1)
                if step.diag is None:
                    pe.wait_ge(bank, 2 * n + 5)
                else:
                    pe.wait_ge(masked, step.g * NB * TT + step.j * TT + step.diag + 1)
                for h in range(HG):
                    last = pe.matmul(ps_o[32 * h:32 * h + 32, step.j % 2, step.w0:], v_pad[:, step.slot, h],
                                     probs[:, step.slot, h, step.w0:], start=step.first, stop=step.last,
                                     tile_position=(0, 32 * h))
                last.then_inc(probs_free, 1)

            def turn_over(g, j):
                pe.wait_ge(o_copied, g * NB + j + 1)
                for t in range(TT):
                    last = pe.transpose(ps_o[:, j % 2, t * P:t * P + P], o_raw[:, t * P:t * P + P], m.ident[:])
                last.then_inc(o_turned, 1)

            def following(step):
                if not step.last:
                    k = step.kt + 1
                    nxt = Step(step.g, step.j, k, 1)
                    nxt.slot = (step.slot + 1) % 3
                    d = None if step.diag is None else step.diag + 1
                    nxt.diag, nxt.w0, nxt.first = d, P * (d or 0), False
                    nxt.count = step.count + 1
                    return nxt
                if step.j == NB - 1:
                    return None
                return Step(step.g, step.j + 1, 0, 0)

            def emit(step):
                score(step, 1)
                nxt = following(step)
                if nxt is not None:
                    score(nxt, 0)
                else:
                    with pe.If(step.g < NG - 1):
                        score(Step(next_group(step.g), 0, 0, 0), 0)
                if not (step.j == 0 and step.first):
                    weigh(preceding(step))
                if step.diag == 2 and step.j > 0:
                    turn_over(step.g, step.j - 1)
                if nxt is None:
                    weigh(step)
                    turn_over(step.g, NB - 1)

            def preceding(step):
                if step.first:
                    return Step(step.g, step.j - 1, TT * step.j - 1, TT * step.j - 1)
                p = Step(step.g, step.j, step.kt - 1, 1)
                p.slot = (step.slot + 2) % 3
                d = None if step.diag is None or step.diag == 0 else step.diag - 1
                p.diag, p.w0 = d, P * (d or 0)
                p.first = step.second
                p.last = False
                p.count = step.count - 1
                return p

            with pe.If(bounded(pe) > 0):
                score(Step(0, 0, 0, 0), 0)
                walk(pe, emit)

        @block.scalar
        def _(act):
            def emit(step):
                act.wait_ge(probs_free, step.count + 1)
                for pair in range(2):
                    u = 2 * step.count + pair
                    act.wait_ge(scored, u + 2)
                    act.activation(probs[:, step.slot, 2 * pair:2 * pair + 2, step.w0:],
                                   ps_s[:, (2 * step.slot + pair) % 3, :, step.w0:], ACT.Exp,
                                   scale=1.0 / DH ** 0.5).then_inc(exped, 1)
                if step.diag == 1 and step.j > 0:
                    copy_out(step.g, step.j - 1)
                if step.j == NB - 1 and step.last:
                    copy_out(step.g, NB - 1)

            def copy_out(g, j):
                act.wait_ge(probs_free, g * STEPS + steps_until(j) + 3)
                act.activation(o_raw, ps_o[:, j % 2], ACT.Copy).then_inc(o_copied, 1)

            with act.If(bounded(act) > 0):
                walk(act, emit)

        @block.vector
        def _(dve):
            dve.sem_inc(bank, 3)
            dve.sem_inc(o_ready, 2)

            def emit(step):
                for pair in range(2):
                    u = 2 * step.count + pair
                    dve.wait_ge(exped, u + 1)
                    p = probs[:, step.slot, 2 * pair:2 * pair + 2, step.w0:]
                    dve.scalar_tensor_tensor(p, ps_s[:, (2 * step.slot + pair) % 3, :, step.w0:], 0.0, p,
                                             ALU.not_equal, ALU.mult).then_inc(bank, 1)
                if step.diag == 3 and step.j > 0:
                    normalise(step.g, step.j - 1)
                if step.j == NB - 1 and step.last:
                    normalise(step.g, NB - 1)

            def normalise(g, j):
                k = g * NB + j
                dve.wait_ge(o_turned, k + 1)
                dve.wait_ge(o_ready, k + 2)
                turned = ps_o[:, j % 2].rearrange("p (a c) -> p a c", a=TT * HG)
                dve.reciprocal(recips.rearrange("p t h -> p (t h)"), turned[:, :, DH]).then_inc(recip_done, 1)
                dve.wait_ge(recip_done, k + 1)
                dve.wait_ge(o_stored[j % 2], 64 * (g * NB // 2 + j // 2) + 16)
                dve.tensor_tensor(o_out[:, j % 2].rearrange("p t h d -> p (t h) d"), turned[:, :, 0:DH],
                                  recips.rearrange("p t (h a) -> p (t h) a", a=1).to_broadcast([P, TT * HG, DH]), ALU.mult)\
                   .then_inc(o_ready, 1)

            with dve.If(bounded(dve) > 0):
                walk(dve, emit)

        @block.gpsimd
        def _(pool):
            pool.memset(v_pad[:, :, :, DH + 1:], 0.0)
            pool.memset(v_pad[:, :, :, DH:DH + 1], 1.0).then_inc(consts, 1)

            def emit(step):
                hold(m, pool, probs_free, step.count + 1)
                src = m.values[:, bass.ds(step.kt, 1), bass.ds(step.g * HG * DH, HG * DH)]
                pool.tensor_copy(v_pad[:, step.slot, :, 0:DH], src.rearrange("p a (h d) -> p (a h) d", h=HG)).then_inc(v_in, 1)
                if step.diag is not None:
                    hold(m, pool, bank, 2 * step.count + 5)
                    sq = probs[:, step.slot, :, step.w0:step.w0 + P]
                    pool.affine_select(out=sq, in_=sq, compare_op=ALU.is_ge, fill=0.0, base=0,
                                       pattern=[[0, HG], [1, P]], channel_multiplier=-1).then_inc(masked, 1)

            with pool.If(bounded(pool) > 0):
                walk(pool, emit)

    nc.clear_and_free_semaphores(own)
    nc.all_engine_barrier()


def phase_attend_unbounded(nc, m):
    UB = NH * TT

    def reused(c0, c):
        return c0 + max(c - 1, 0)

    with ExitStack() as ctx:
        def sem(name):
            return ctx.enter_context(nc.semaphore("u_" + name))

        a = Carver(m.arena2)
        row = a.take(NB, BT)
        keep = a.take(TT, BT)
        q_stack = a.take(BT, dt=BF16)
        hidden = a.take(BT)
        turned_p = a.take(2, TT, P)
        tops = a.take(NB)
        top, shift, alive, total, inverse = (a.take(1) for _ in range(5))
        o_out = a.take(DH)
        ps_s = ctx.enter_context(nc.psum_tensor("u_ps_s", [P, 2, BT], F32))
        ps_t = ctx.enter_context(nc.psum_tensor("u_ps_t", [P, 2, TT, P], F32))
        ps_o = ctx.enter_context(nc.psum_tensor("u_ps_o", [P, BT], F32))
        k_in, q_in, q_used, kept, scored, copied = (sem("k_in"), sem("q_in"), sem("q_used"), sem("kept"), sem("scored"), sem("copied"))
        maxed, exped, turned, taken, weighed, o_ready = (sem("maxed"), sem("exped"), sem("turned"), sem("taken"),
                                                         sem("weighed"), sem("o_ready"))
        chain, stored, all_kept = sem("chain"), sem("stored"), sem("all_kept")
        block = ctx.enter_context(nc.Block())

        def unbounded(eng):
            return eng.If(eng.value_load(m.bounded[0:1, 0:1], min_val=0, max_val=1) < 1)

        def units(eng, unit, start=None, finish=None):
            for j in range(NB):
                before, chunks = UB * j, UB * (j * (j + 1) // 2)
                with eng.Fori(0, NH) as h:
                    if start is not None:
                        start(j, h)
                    with eng.Fori(0, TT) as t:
                        unit(j, h, t, before + TT * h + t, chunks + (j + 1) * (TT * h + t))
                    if finish is not None:
                        finish(j, h)

        @block.sync
        def _(sp):
            with unbounded(sp):
                wait_parts_stored(m, sp)
                load_first_k(m, sp, NB - 1, m.kload_last)
                for r in range(8):
                    sp.dma_start(m.k_stack[DH * r:DH * r + DH, HG:NH, :],
                                 m.parts[1, K_PART[r], HG * DH:D, :].rearrange("(h d) n -> d h n", d=DH)).then_inc(k_in, 16)

                def load(j, h):
                    hold(m, sp, q_used, NH * j + h + 1)
                    for r in range(8):
                        sp.dma_start(q_stack[DH * r:DH * r + DH, :],
                                     m.parts[0, Q_PART[r], bass.ds(h * DH, DH), j * BT:j * BT + BT]).then_inc(q_in, 16)

                def store(j, h, t, n, c0):
                    hold(m, sp, o_ready, n + 2)
                    sp.dma_start(m.attn[bass.ds(t * P + j * BT, P), bass.ds(h * DH, DH)], o_out).then_inc(stored, 16)

                units(sp, store, load)
                sp.wait_ge(stored, 16 * (UB * NB + 1))
                load_weights(m, sp)
                clear_slots(m, sp)

        @block.gpsimd
        def _(pool):
            with unbounded(pool):
                pool.memset(keep, 1.0).then_inc(kept, 1)
                pool.wait_ge(kept, 1)
                for t in range(TT):
                    last = pool.affine_select(out=keep[:, t], in_=keep[:, t], compare_op=ALU.is_ge, fill=0.0, base=P * t,
                                              pattern=[[-1, BT]], channel_multiplier=1)
                last.then_inc(all_kept, 1)

        @block.tensor
        def _(pe):
            with unbounded(pe):
                pe.sem_inc(turned, 1)
                pe.sem_inc(weighed, 1)
                pe.sem_inc(q_used, 1)
                pe.wait_ge(m.kload_first, 16 * 8 * (NB - 1))
                pe.wait_ge(m.kload_last, 128)
                pe.wait_ge(k_in, 128)

                def unit(j, h, t, n, c0):
                    pe.wait_ge(q_in, 128 * (NH * j + h + 1))
                    for c in range(j + 1):
                        pe.wait_ge(copied, reused(c0, c) + 1)
                        last = pe.matmul(ps_s[:, c % 2], q_stack[:, bass.ds(t * P, P)],
                                         m.k_stack[:, bass.ds(h, 1), c * BT:c * BT + BT].rearrange("p a n -> p (a n)"),
                                         start=True, stop=True).then_inc(scored, 1)
                    pe.wait_ge(exped, n + 2)
                    for c in range(j + 2):
                        if c <= j:
                            pe.wait_ge(taken, reused(c0, c) + 1)
                            for i in range(TT):
                                last = pe.transpose(ps_t[:, c % 2, i], row[:, c, i * P:i * P + P], m.ident[:])
                            last.then_inc(turned, 1)
                        if c > 0:
                            pe.wait_ge(taken, c0 + c + 1)
                            pe.wait_ge(o_ready, n + 1)
                            for i in range(TT):
                                last = pe.matmul(ps_o[:, 0:DH], turned_p[:, (c - 1) % 2, i],
                                                 m.values[:, TT * (c - 1) + i, bass.ds(h * DH, DH)],
                                                 start=c == 1 and i == 0, stop=c == j + 1 and i == TT - 1)
                            last.then_inc(weighed, 1)

                def finish(j, h):
                    pe.wait_ge(weighed, UB * (j * (j + 1) // 2) + (j + 1) * TT * (h + 1) + 1)
                    pe.sem_inc(q_used, 1)

                units(pe, unit, finish=finish)

        @block.scalar
        def _(act):
            with unbounded(act):
                act.sem_inc(exped, 1)
                act.sem_inc(taken, 1)

                def unit(j, h, t, n, c0):
                    act.wait_ge(maxed, n + 1)
                    act.activation(row[:, 0:j + 1], row[:, 0:j + 1], ACT.Exp, bias=shift).then_inc(exped, 1)
                    for c in range(j + 1):
                        act.wait_ge(turned, c0 + c + 2)
                        act.wait_ge(weighed, reused(c0, c) + 1)
                        act.activation(turned_p[:, c % 2], ps_t[:, c % 2], ACT.Copy).then_inc(taken, 1)

                units(act, unit)

        @block.vector
        def _(dve):
            with unbounded(dve):
                dve.sem_inc(copied, 1)
                dve.sem_inc(o_ready, 1)
                dve.sem_inc(stored, 16)
                dve.wait_ge(all_kept, 1)

                def unit(j, h, t, n, c0):
                    steps = 3 * (j + 1) + 6
                    done = sum(3 * (i + 1) + 6 for i in range(j)) * UB + steps * (TT * h + t)
                    k = 0

                    def link(ins):
                        nonlocal k
                        k += 1
                        ins.then_inc(chain, 1)
                        dve.wait_ge(chain, done + k)

                    dve.wait_ge(turned, c0 + 1)
                    for c in range(j + 1):
                        dve.wait_ge(scored, c0 + c + 1)
                        if c < j:
                            dve.tensor_scalar(row[:, c], ps_s[:, c % 2], 1.0 / DH ** 0.5, None, ALU.mult).then_inc(copied, 1)
                        else:
                            dve.scalar_tensor_tensor(row[:, c], ps_s[:, c % 2], 1.0 / DH ** 0.5,
                                                     keep[:, bass.ds(t, 1)].rearrange("p a n -> p (a n)"),
                                                     ALU.mult, ALU.mult).then_inc(copied, 1)
                        dve.wait_ge(copied, c0 + c + 2)
                        link(dve.tensor_scalar(hidden, row[:, c], 0.0, -BIG, ALU.is_equal, ALU.mult))
                        link(dve.tensor_tensor(row[:, c], row[:, c], hidden, ALU.add))
                        link(dve.tensor_reduce(tops[:, c:c + 1], row[:, c], AX.X, ALU.max))
                    link(dve.tensor_reduce(top, tops[:, 0:j + 1], AX.X, ALU.max))
                    link(dve.tensor_scalar(alive, top, -BIG, None, ALU.is_gt))
                    link(dve.tensor_scalar(shift, top, -1.0, None, ALU.mult))
                    dve.sem_inc(maxed, 1)
                    dve.wait_ge(exped, n + 2)
                    link(dve.tensor_reduce(total, row[:, 0:j + 1], AX.XY, ALU.add))
                    link(dve.tensor_scalar(total, total, alive, None, ALU.mult))
                    link(dve.reciprocal(inverse, total))
                    dve.wait_ge(weighed, c0 + j + 2)
                    dve.wait_ge(stored, 16 * (n + 1))
                    dve.tensor_scalar(o_out, ps_o[:, 0:DH], alive, inverse, ALU.mult, ALU.mult).then_inc(o_ready, 1)

                units(dve, unit)


class LayerNorm:

    def __init__(self, nc, m, ctx, name, a, own=True):
        self.m = m
        self.stats = a.take(2, TT, 6)
        self.mv = a.take(2, TT, 2)
        self.ve = a.take(2, TT)
        self.rstd = a.take(2, TT)
        if own:
            self.xn = a.take(2, TT, D)
            self.ps = ctx.enter_context(nc.psum_tensor(name + "_ps", [P, KC, BT], F32))
        self.st, self.mvs, self.added, self.rst, self.normed, self.turned, self.taken = (
            ctx.enter_context(nc.semaphore(name + "_" + s)) for s in ("st", "mvs", "added", "rst", "normed", "turned", "taken"))

    def statistics(self, dve, b, s, tiles, ready, count):
        hold(self.m, dve, ready, count)
        for t in range(TT):
            last = dve.bn_stats(self.stats[:, s, t], tiles[:, t])
        last.then_inc(self.st, 1)
        hold(self.m, dve, self.st, b + 1)
        for t in range(TT):
            last = dve.bn_aggr(self.mv[:, s, t], self.stats[:, s, t])
        last.then_inc(self.mvs, 1)

    def inverse_deviation(self, pool, b, s):
        hold(self.m, pool, self.mvs, b + 1)
        pool.tensor_scalar(self.ve[:, s], self.mv[:, s, :, 1], EPS, None, ALU.add).then_inc(self.added, 1)
        hold(self.m, pool, self.added, b + 1)
        pool.tensor_tensor(self.rstd[:, s], self.ve[:, s], self.m.mhalf[:], ALU.pow).then_inc(self.rst, 1)

    def normalise(self, dve, b, s, tiles, out=None):
        dve.wait_ge(self.rst, b + 1)
        for t in range(TT):
            last = dve.tensor_scalar((self.xn[:, s] if out is None else out)[:, t], tiles[:, t], self.mv[:, s, t, 0:1],
                                     self.rstd[:, s, t:t + 1], ALU.subtract, ALU.mult)
        last.then_inc(self.normed, 1)

    def transposes(self, pe, b, s):
        pe.wait_ge(self.normed, b + 1)
        pe.wait_ge(self.taken, b + 1)
        for k in range(KC):
            for t in range(TT):
                last = pe.transpose(self.ps[:, k, t * P:t * P + P], self.xn[:, s, t, k * P:k * P + P], self.m.ident[:])
        last.then_inc(self.turned, 1)

    def modulate(self, act, b, s, out, layer, shift, scale):
        act.wait_ge(self.turned, b + 3)
        for k in range(KC):
            last = act.activation(out[:, k], self.ps[:, k], ACT.Identity, bias=self.m.mod_cols[:, layer, shift, k:k + 1],
                                  scale=self.m.mod_cols[:, layer, scale, k:k + 1])
        last.then_inc(self.taken, 1)


def phase_weights(nc, m):
    with ExitStack() as ctx:
        def sem(name):
            return ctx.enter_context(nc.semaphore("w_" + name))

        sums = Carver(m.arena2).take(2, KC, NH)
        chain, zeroed = sem("chain"), sem("zeroed")
        block = ctx.enter_context(nc.Block())

        @block.vector
        def _(dve):
            steps = [0]

            def link(ins):
                steps[0] += 1
                ins.then_inc(chain, 1)
                dve.wait_ge(chain, steps[0])

            dve.wait_ge(m.weights_in, m.weights_expected)
            for k in range(KC):
                dve.tensor_tensor(m.w_o[:, k], m.w_o[:, k], m.gates[:, 0, 0], ALU.mult)
                dve.tensor_tensor(m.w_v[:, k], m.w_v[:, k], m.gates[:, 0, 1], ALU.mult)
            for n, w in enumerate((m.l1_q, m.l1_v)):
                link(dve.tensor_reduce(sums[:, n], w.rearrange("p k (h d) -> p k h d", d=DH), AX.X, ALU.add))
            for k in range(KC):
                for src, w in ((sums[:, 0, k], m.l1_q), (sums[:, 1, k], m.l1_v), (m.beta_narrow[:, k], m.l1_beta)):
                    dve.tensor_copy(w[:, k].rearrange("p (h d) -> p h d", d=DH),
                                    src.rearrange("p (h a) -> p h a", a=1).to_broadcast([P, NH, DH]))
            dve.tensor_tensor(m.ln_gain, m.ln_gain, m.gates[:, 1, 0], ALU.mult)
            dve.tensor_tensor(m.ln_shift, m.ln_shift, m.gates[:, 1, 0], ALU.mult)
            dve.tensor_tensor(m.b_o, m.b_o, m.mod_rows[:, 0], ALU.add)
            for k, (_, rows) in enumerate(FM):
                link(dve.tensor_tensor(m.s_down[0:rows, k], m.s_down[0:rows, k], m.gates[0:rows, 1, 1], ALU.mult))

        @block.gpsimd
        def _(pool):
            pool.memset(m.mhalf[:], -0.5)
            pool.memset(m.h_even[:, :, 0:1], 0.0).then_inc(zeroed, 1)
            pool.wait_ge(zeroed, 1)


def phase_attend_out(nc, m):
    with ExitStack() as ctx:
        def sem(name):
            return ctx.enter_context(nc.semaphore("c_" + name))

        a = Carver(m.arena2)
        attn = a.take(2, TT, D)
        attnT = a.take(2, KC, BT)
        ln = LayerNorm(nc, m, ctx, "c_ln", a)
        ps_a = ctx.enter_context(nc.psum_tensor("c_ps_a", [P, KC, BT], F32))
        ps_o = ctx.enter_context(nc.psum_tensor("c_ps_o", [P, 2, 2 * D], F32))
        a_in = [sem("a_in0"), sem("a_in1")]
        turned, taken, summed, added = sem("turned"), sem("taken"), sem("summed"), sem("added")
        x_dram = m.ins["L0_attn_x"].rearrange("a (b t p) d -> p (a b) t d", p=P, t=TT)
        a_dram = m.attn.rearrange("(b t p) n -> p b t n", p=P, t=TT)
        block = ctx.enter_context(nc.Block())

        @block.sync
        def _(sp):
            def load(b, s, h):
                hold(m, sp, turned, b + 1)
                sp.dma_start(attn[:, s], pick(a_dram, b)).then_inc(a_in[s], 16)
                sp.dma_start(m.x[:, bass.ds(b * TT, TT)], pick(x_dram, b)).then_inc(a_in[s], 16)

            pipeline(sp, [(0, load)])

        @block.tensor
        def _(pe):
            pe.sem_inc(turned, 2)
            pe.sem_inc(summed, 4)
            pe.sem_inc(ln.turned, 2)

            def turn_attn(b, s, h):
                pe.wait_ge(a_in[s], 32 * (h + 1))
                pe.wait_ge(taken, b + 1)
                for k in range(KC):
                    for t in range(TT):
                        last = pe.transpose(ps_a[:, k, t * P:t * P + P], attn[:, s, t, k * P:k * P + P], m.ident[:])
                last.then_inc(turned, 1)

            def out(b, s, h):
                pe.wait_ge(taken, b + 2)
                for c in range(2):
                    pe.wait_ge(added, 2 * b + c + 1)
                    for t in range(2):
                        at = (2 * c + t) * P
                        for k in range(KC):
                            last = pe.matmul(ps_o[:, c, t * D:t * D + D], attnT[:, s, k, at:at + P], m.w_o[:, k],
                                             start=k == 0, stop=k == KC - 1)
                    last.then_inc(summed, 1)

            pipeline(pe, [(0, turn_attn), (1, out), (3, lambda b, s, h: ln.transposes(pe, b, s))])

        @block.scalar
        def _(act):
            act.sem_inc(taken, 1)
            act.sem_inc(ln.taken, 1)

            def take_attn(b, s, h):
                act.wait_ge(turned, b + 3)
                act.wait_ge(summed, 2 * b + 2)
                act.activation(attnT[:, s], ps_a[:], ACT.Copy).then_inc(taken, 1)

            def modulate(b, s, h):
                ln.modulate(act, b, s, m.h_even[:, :, bass.ds(b * BT + 1, BT)], 0, 2, 3)

            pipeline(act, [(0, take_attn), (3, modulate)])

        @block.vector
        def _(dve):
            dve.sem_inc(added, 2)

            def add(b, s, h):
                dve.wait_ge(a_in[s], 32 * (h + 1))
                for c in range(2):
                    dve.wait_ge(summed, 2 * b + c + 5)
                    x = m.x[:, bass.ds(b * TT + 2 * c, 2)]
                    dve.tensor_tensor(x, ps_o[:, c].rearrange("p (t n) -> p t n", t=2), x, ALU.add).then_inc(added, 1)
                tiles = m.x[:, bass.ds(b * TT, TT)]
                ln.statistics(dve, b, s, tiles, added, 2 * b + 4)

            def normalise(b, s, h):
                dve.wait_ge(ln.turned, b + 1)
                ln.normalise(dve, b, s, m.x[:, bass.ds(b * TT, TT)])

            pipeline(dve, [(1, normalise), (0, add)])

        @block.gpsimd
        def _(pool):
            pipeline(pool, [(0, lambda b, s, h: ln.inverse_deviation(pool, b, s))])


def phase_channel_mix(nc, m):
    with ExitStack() as ctx:
        def sem(name):
            return ctx.enter_context(nc.semaphore("d_" + name))

        def pb(name, shape):
            return ctx.enter_context(nc.psum_tensor("d_" + name, shape, F32))

        a = Carver(m.arena2)
        xr = a.take(2, KC, BT)
        xk = a.take(2, KC, BT)
        act_k = a.take(KC, BT)
        gate = a.take(2, 2 * D)
        ln = LayerNorm(nc, m, ctx, "d_ln", a)
        ps_r, ps_k, ps_kv = pb("ps_r", [P, 2, 2 * D]), pb("ps_k", [P, KC, BT]), pb("ps_kv", [P, 2, 2 * D])
        stepped, mixed_r, mixed_k, r_done, k_done = sem("stepped"), sem("mixed_r"), sem("mixed_k"), sem("r_done"), sem("k_done")
        gated, relued, squared, kv_done, multiplied, added = (sem("gated"), sem("relued"), sem("squared"), sem("kv_done"),
                                                              sem("multiplied"), sem("added"))
        hrow, hrow_chain = sem("hrow"), sem("hrow_chain")
        block = ctx.enter_context(nc.Block())

        @block.gpsimd
        def _(pool):
            pool.sem_inc(squared, 1)
            pool.sem_inc(hrow, 2)

            def difference(b, s, h):
                hold(m, pool, r_done, 2 * b + 1)
                pool.tensor_tensor(xr[:, s], m.h_even[:, :, bass.ds(b * BT + 1, BT)], m.h_even[:, :, bass.ds(b * BT, BT)],
                                   ALU.subtract).then_inc(stepped, 1)

            def square(b, s, h):
                hold(m, pool, relued, b + 2)
                pool.tensor_tensor(act_k, act_k, act_k, ALU.mult).then_inc(squared, 1)

            def rows(b, s, h):
                hold(m, pool, ln.normed, b + 1)
                wide = [P, TT, D]
                scale = m.mod_rows[:, 1:2].to_broadcast(wide)
                shift = m.b_o.rearrange("p (a n) -> p a n", a=1).to_broadcast(wide)
                out = m.h_rows[:, bass.ds(b * TT, TT)]
                pool.tensor_tensor(out, ln.xn[:, s], scale, ALU.mult).then_inc(hrow_chain, 1)
                hold(m, pool, hrow_chain, b + 1)
                pool.tensor_tensor(out, out, shift, ALU.add).then_inc(hrow, 1)

            pipeline(pool, [(0, difference), (2, lambda b, s, h: ln.inverse_deviation(pool, b, s)), (1, square), (2, rows)])

        @block.vector
        def _(dve):
            dve.sem_inc(mixed_k, 1)
            dve.sem_inc(added, 2)
            dve.sem_inc(multiplied, 2)

            def mix(b, s, h):
                dve.wait_ge(stepped, b + 1)
                dve.wait_ge(k_done, 2 * b + 1)
                for k in range(KC):
                    last = dve.scalar_tensor_tensor(xk[:, s, k], xr[:, s, k], m.mu[:, 1, k:k + 1],
                                                    m.h_even[:, k, bass.ds(b * BT, BT)], ALU.mult, ALU.add)
                last.then_inc(mixed_k, 1)
                dve.wait_ge(mixed_k, b + 2)
                for k in range(KC):
                    last = dve.scalar_tensor_tensor(xr[:, s, k], xr[:, s, k], m.mu[:, 0, k:k + 1],
                                                    m.h_even[:, k, bass.ds(b * BT, BT)], ALU.mult, ALU.add)
                last.then_inc(mixed_r, 1)

            def combine(b, s, h):
                for c in range(2):
                    dve.wait_ge(gated, 2 * b + c + 2)
                    dve.wait_ge(kv_done, 2 * b + c + 2)
                    dve.tensor_tensor(gate[:, c], ps_kv[:, c], gate[:, c], ALU.mult).then_inc(multiplied, 1)
                    dve.wait_ge(multiplied, 2 * b + c + 3)
                    x = m.x[:, bass.ds(b * TT + 2 * c, 2)]
                    dve.tensor_tensor(x, gate[:, c].rearrange("p (t n) -> p t n", t=2), x, ALU.add).then_inc(added, 1)
                tiles = m.x[:, bass.ds(b * TT, TT)]
                ln.statistics(dve, b, s, tiles, added, 2 * b + 4)

            def normalise(b, s, h):
                dve.wait_ge(ln.turned, b + 1)
                dve.wait_ge(hrow, b + 1)
                ln.normalise(dve, b, s, m.x[:, bass.ds(b * TT, TT)])

            pipeline(dve, [(2, combine), (0, mix), (2, normalise)])

        @block.scalar
        def _(act):
            act.sem_inc(gated, 1)
            act.sem_inc(relued, 1)
            act.sem_inc(ln.taken, 1)

            def gate_(b, s, h):
                for c in range(2):
                    act.wait_ge(r_done, 2 * b + c + 4)
                    act.wait_ge(added, 2 * b + c + 1)
                    act.activation(gate[:, c], ps_r[:, c], ACT.Sigmoid).then_inc(gated, 1)

            def rectify(b, s, h):
                act.wait_ge(k_done, 2 * b + 5)
                act.wait_ge(kv_done, 2 * b + 1)
                act.activation(act_k, ps_k[:], ACT.Relu).then_inc(relued, 1)

            def modulate(b, s, h):
                ln.modulate(act, b, s, m.h_odd[:, :, bass.ds(b * BT, BT)], 1, 0, 1)

            pipeline(act, [(1, rectify), (1, gate_), (3, modulate)])

        @block.tensor
        def _(pe):
            pe.sem_inc(r_done, 3)
            pe.sem_inc(k_done, 3)
            pe.sem_inc(kv_done, 1)
            pe.sem_inc(ln.turned, 2)

            def gates(b, s, h):
                pe.wait_ge(mixed_r, b + 1)
                pe.wait_ge(gated, 2 * b + 1)
                for c in range(2):
                    for t in range(2):
                        at = (2 * c + t) * P
                        for k in range(KC):
                            last = pe.matmul(ps_r[:, c, t * D:t * D + D], xr[:, s, k, at:at + P], m.w_r[:, k],
                                             start=k == 0, stop=k == KC - 1)
                    last.then_inc(r_done, 1)

            def keys(b, s, h):
                pe.wait_ge(mixed_k, b + 2)
                pe.wait_ge(relued, b + 1)
                for mm in range(KC):
                    for k in range(KC):
                        last = pe.matmul(ps_k[:, mm], m.w_k[:, k, mm * P:mm * P + P], xk[:, s, k], start=k == 0, stop=k == KC - 1)
                    last.then_inc(k_done, 1)

            def values(b, s, h):
                pe.wait_ge(squared, b + 2)
                pe.wait_ge(multiplied, 2 * b + 1)
                for c in range(2):
                    if c == 1:
                        pe.wait_ge(multiplied, 2 * b + 2)
                    for t in range(2):
                        at = (2 * c + t) * P
                        for k in range(KC):
                            last = pe.matmul(ps_kv[:, c, t * D:t * D + D], act_k[:, k, at:at + P], m.w_v[:, k],
                                             start=k == 0, stop=k == KC - 1)
                    last.then_inc(kv_done, 1)

            pipeline(pe, [(2, values), (1, keys), (1, gates), (3, lambda b, s, h: ln.transposes(pe, b, s))])


def phase_delta(nc, m):
    with ExitStack() as ctx:
        def sem(name):
            return ctx.enter_context(nc.semaphore("e_" + name))

        def pb(name, shape):
            return ctx.enter_context(nc.psum_tensor("e_" + name, shape, F32))

        a = Carver(m.arena2)
        keys = a.take(KC, BT)
        beta = a.take(KC, BT)
        state = a.take(KC, BT)
        o_t = a.take(KC, BT)
        ln2 = LayerNorm(nc, m, ctx, "e_ln2", a)
        y = [a.take(TT, D)]
        y.append(a.take(TT, D))
        carry = a.take(KC)
        ln1 = LayerNorm(nc, m, ctx, "e_ln1", a, own=False)
        ps_k, ps_v, ps_b, ps_q = pb("ps_k", [P, BT]), pb("ps_v", [P, BT]), pb("ps_b", [P, BT]), pb("ps_q", [P, BT])
        ps_y = pb("ps_y", [P, 2, 2 * D])
        k_done, v_done, b_done, q_done = sem("k_done"), sem("v_done"), sem("b_done"), sem("q_done")
        k_copied, v_used, beta_made, q_used = sem("k_copied"), sem("v_used"), sem("beta_made"), sem("q_used")
        scanned, carried, y_done, y_added, scaled, gained = (sem("scanned"), sem("carried"), sem("y_done"), sem("y_added"),
                                                             sem("scaled"), sem("gained"))
        x_done, row_chain, rows_done = sem("x_done"), sem("row_chain"), sem("rows_done")
        block = ctx.enter_context(nc.Block())

        @block.tensor
        def _(pe):
            pe.sem_inc(y_done, 2)
            pe.sem_inc(ln2.turned, 2)

            def project(b, c):
                n = 2 * b + c
                for ps, w, free, at, done in ((ps_k, m.l1_k, k_copied, n + 1, k_done), (ps_v, m.l1_v, v_used, n + 2, v_done),
                                              (ps_b, m.l1_beta, beta_made, n + 1, b_done), (ps_q, m.l1_q, q_used, n + 1, q_done)):
                    pe.wait_ge(free, at)
                    for k in range(KC):
                        last = pe.matmul(ps[:, :], w[:, k, c * P:c * P + P], m.h_odd[:, k, bass.ds(b * BT, BT)],
                                         start=k == 0, stop=k == KC - 1)
                    last.then_inc(done, 1)

            def out(b, s, h):
                pe.wait_ge(q_used, 2 * b + 3)
                for c in range(2):
                    pe.wait_ge(y_added, 2 * b + c + 1)
                    for t in range(2):
                        at = (2 * c + t) * P
                        for k in range(KC):
                            last = pe.matmul(ps_y[:, c, t * D:t * D + D], o_t[:, k, at:at + P], m.l1_o[:, k],
                                             start=k == 0, stop=k == KC - 1)
                    last.then_inc(y_done, 1)

            pipeline(pe, [(0, lambda b, s, h: project(b, 0)), (1, out), (0, lambda b, s, h: project(b, 1)),
                          (3, lambda b, s, h: ln2.transposes(pe, b, s))])

        @block.scalar
        def _(act):
            act.sem_inc(k_copied, 1)
            act.sem_inc(beta_made, 1)
            act.sem_inc(ln2.taken, 1)

            def take(b, s, h):
                for c in range(KC):
                    n = 2 * b + c
                    act.wait_ge(k_done, n + 1)
                    act.wait_ge(scanned, n + 1)
                    act.activation(keys[:, c], ps_k[:, :], ACT.Copy).then_inc(k_copied, 1)
                    act.wait_ge(b_done, n + 1)
                    act.activation(beta[:, c], ps_b[:, :], ACT.Sigmoid, bias=m.b_beta[:, c:c + 1]).then_inc(beta_made, 1)

            def modulate(b, s, h):
                ln2.modulate(act, b, s, m.h_even[:, :, bass.ds(b * BT, BT)], 1, 2, 3)

            pipeline(act, [(0, take), (3, modulate)])

        @block.vector
        def _(dve):
            dve.sem_inc(v_used, 2)
            dve.sem_inc(scanned, 2)
            dve.sem_inc(q_used, 1)
            dve.sem_inc(y_added, 2)
            dve.sem_inc(carried, 2)

            def scan(b, c):
                n = 2 * b + c
                dve.wait_ge(k_copied, n + 2)
                dve.wait_ge(v_done, n + 1)
                dve.tensor_tensor(keys[:, c], ps_v[:, :], keys[:, c], ALU.mult).then_inc(v_used, 1)
                dve.wait_ge(v_used, n + 3)
                dve.wait_ge(beta_made, n + 2)
                dve.wait_ge(carried, n + 1)
                start = 0.0 if isinstance(b, int) and b == 0 else carry[:, c:c + 1]
                dve.tensor_tensor_scan(state[:, c], beta[:, c], keys[:, c], start, ALU.mult, ALU.add).then_inc(scanned, 1)
                dve.wait_ge(scanned, n + 3)
                dve.tensor_copy(carry[:, c:c + 1], state[:, c, BT - 1:BT]).then_inc(carried, 1)
                dve.wait_ge(q_done, n + 1)
                dve.wait_ge(y_done, 2 * b + 2)
                dve.tensor_tensor(o_t[:, c], ps_q[:, :], state[:, c], ALU.mult).then_inc(q_used, 1)

            def residual(b, s, h):
                for c in range(2):
                    dve.wait_ge(y_done, 2 * b + c + 3)
                    dve.tensor_tensor(y[s][:, 2 * c:2 * c + 2], ps_y[:, c].rearrange("p (t n) -> p t n", t=2),
                                      m.h_rows[:, bass.ds(b * TT + 2 * c, 2)], ALU.add).then_inc(y_added, 1)
                ln1.statistics(dve, b, s, y[s], y_added, 2 * b + 4)

            def add(b, s, h):
                x = m.x[:, bass.ds(b * TT, TT)]
                dve.wait_ge(gained, b + 1)
                dve.tensor_tensor(x, y[s], x, ALU.add).then_inc(x_done, 1)
                ln2.statistics(dve, b, s, x, x_done, b + 1)

            def normalise(b, s, h):
                dve.wait_ge(ln2.turned, b + 1)
                dve.wait_ge(rows_done, b + 1)
                ln2.normalise(dve, b, s, m.x[:, bass.ds(b * TT, TT)])

            pipeline(dve, [(0, lambda b, s, h: scan(b, 0)), (1, residual), (2, add), (0, lambda b, s, h: scan(b, 1)),
                           (1, lambda b, s, h: ln1.normalise(dve, b, s, y[s], out=y[s])), (2, normalise)])

        @block.gpsimd
        def _(pool):
            pool.sem_inc(rows_done, 2)
            wide = [P, TT, D]

            def over_tiles(row):
                return row.rearrange("p (a n) -> p a n", a=1).to_broadcast(wide)

            def gain(b, s, h):
                hold(m, pool, ln1.normed, b + 1)
                pool.tensor_tensor(y[s], y[s], over_tiles(m.ln_gain), ALU.mult).then_inc(scaled, 1)
                hold(m, pool, scaled, b + 1)
                pool.tensor_tensor(y[s], y[s], over_tiles(m.ln_shift), ALU.add).then_inc(gained, 1)

            def rows(b, s, h):
                hold(m, pool, ln2.normed, b + 1)
                out = m.h_rows[:, bass.ds(b * TT, TT)]
                pool.tensor_tensor(out, ln2.xn[:, s], over_tiles(m.mod_rows[:, 3]), ALU.mult).then_inc(row_chain, 1)
                hold(m, pool, row_chain, b + 1)
                pool.tensor_tensor(out, out, over_tiles(m.mod_rows[:, 2]), ALU.add).then_inc(rows_done, 1)

            pipeline(pool, [(1, lambda b, s, h: ln1.inverse_deviation(pool, b, s)),
                            (2, lambda b, s, h: ln2.inverse_deviation(pool, b, s)), (1, gain), (2, rows)])


def phase_route(nc, m):
    NS = NT * E_
    with ExitStack() as ctx:
        def sem(name):
            return ctx.enter_context(nc.semaphore("g_" + name))

        a = Carver(m.arena, m.odd_at)

        def tile():
            return a.take(NT, E_)

        shifted, expd, prob, hit, rank, one1, one2, left = (tile() for _ in range(8))
        pos, dest, pick_, weigh_ = (tile() for _ in range(4))
        totals, running, keep = a.take(E_, NT), a.take(E_, NT), a.take(E_, NT)
        a = Carver(m.arena2)
        top, total, inv, best1, best2, v1, v2 = (a.take(NT) for _ in range(7))
        den, where, place, inside, miss = (a.take(2, NT) for _ in range(5))
        mask = a.take(NT, E_, dt=BF16)
        lower = a.take(P, dt=BF16)
        ones = a.take(P, dt=BF16)
        lower_f, ones_f = a.take(P), a.take(P)
        backward, base = a.take(E_), a.take(E_)
        m.route_weight = m.logits[:, 0:4].rearrange("p t e -> p (t e)").rearrange("p (k t) -> p k t", k=2)
        ps_l = ctx.enter_context(nc.psum_tensor("g_ps_l", [P, NS], F32))
        ps_w = ctx.enter_context(nc.psum_tensor("g_ps_w", [P, NS], F32))
        ps_t = ctx.enter_context(nc.psum_tensor("g_ps_t", [P, NS], F32))
        loaded, logits_done, maxed, exped, masked, counted, chain = map(
            sem, ["loaded", "logits_done", "maxed", "exped", "masked", "counted", "chain"])
        block = ctx.enter_context(nc.Block())

        def wide(col):
            return col.rearrange("p (t a) -> p t a", a=1).to_broadcast([P, NT, E_])

        def rows(row):
            return row.rearrange("p (a e) -> p a e", a=1).to_broadcast([P, NT, E_])

        @block.sync
        def _(sp):
            for dst, name in ((lower_f, "earlier"), (keep.rearrange("p e t -> p (e t)"), "keep_run"),
                              (backward, "backward"), (base, "slot_base")):
                sp.dma_start(dst, m.ins[name]).then_inc(loaded, 16)
            sp.wait_ge(loaded, 64)

        @block.scalar
        def _(act):
            act.wait_ge(maxed, 1)
            act.activation(expd, shifted, ACT.Exp).then_inc(exped, 1)

        @block.tensor
        def _(pe):
            for t in range(NT):
                for k in range(KC):
                    last = pe.matmul(ps_l[:, t * E_:t * E_ + E_], m.h_even[:, k, t * P:t * P + P], m.router[:, k],
                                     start=k == 0, stop=k == KC - 1)
            last.then_inc(logits_done, 1)
            pe.wait_ge(masked, 1)
            mk = mask.rearrange("p t e -> p (t e)")
            pe.matmul(ps_w[:, :], lower, mk, start=True, stop=True)
            pe.matmul(ps_t[:, :], ones, mk, start=True, stop=True).then_inc(counted, 1)

        @block.vector
        def _(dve):
            steps = [0]

            def link(ins):
                steps[0] += 1
                ins.then_inc(chain, 1)
                dve.wait_ge(chain, steps[0])

            dve.memset(ones_f, 1.0)
            dve.wait_ge(loaded, 64)
            link(dve.tensor_copy(lower, lower_f))
            link(dve.tensor_copy(ones, ones_f))
            dve.wait_ge(logits_done, 1)
            link(dve.tensor_tensor(m.logits, ps_l[:, :].rearrange("p (t e) -> p t e", e=E_), rows(m.router_b), ALU.add))
            link(dve.tensor_reduce(top, m.logits, AX.X, ALU.max))
            dve.tensor_tensor(shifted, m.logits, wide(top), ALU.subtract).then_inc(maxed, 1)
            dve.wait_ge(exped, 1)
            link(dve.tensor_reduce(total, expd, AX.X, ALU.add))
            link(dve.reciprocal(inv, total))
            link(dve.tensor_tensor(prob, expd, wide(inv), ALU.mult))
            left_over = prob
            for best, value, one in ((best1, v1, one1), (best2, v2, one2)):
                link(dve.tensor_reduce(value, left_over, AX.X, ALU.max))
                link(dve.tensor_tensor(hit, left_over, wide(value), ALU.is_equal))
                link(dve.tensor_tensor(rank, hit, rows(backward), ALU.mult))
                link(dve.tensor_reduce(best, rank, AX.X, ALU.max))
                link(dve.tensor_tensor(one, rows(backward), wide(best), ALU.is_equal))
                if best is best1:
                    link(dve.scalar_tensor_tensor(left, one, -2.0, prob, ALU.mult, ALU.add))
                    left_over = left
            dve.tensor_tensor(mask, one1, one2, ALU.add).then_inc(masked, 1)
            link(dve.tensor_tensor(den[:, 0], v1, v2, ALU.add))
            link(dve.tensor_scalar(den[:, 0], den[:, 0], 1e-9, None, ALU.add))
            link(dve.reciprocal(den[:, 1], den[:, 0]))
            link(dve.tensor_tensor(weigh_[:, 0:2].rearrange("p t e -> p (t e)"), v1, den[:, 1], ALU.mult))
            link(dve.tensor_tensor(weigh_[:, 2:4].rearrange("p t e -> p (t e)"), v2, den[:, 1], ALU.mult))
            dve.wait_ge(counted, 1)
            link(dve.tensor_copy(totals, ps_t[:, :].rearrange("p (t e) -> p e t", e=E_)))
            flat = [v.rearrange("p e t -> p (e t)") for v in (running, keep, totals)]
            link(dve.tensor_tensor_scan(*flat, 0.0, ALU.mult, ALU.add))
            link(dve.tensor_tensor(running, running, totals, ALU.subtract))
            link(dve.tensor_tensor(pos, ps_w[:, :].rearrange("p (t e) -> p t e", e=E_), running.rearrange("p e t -> p t e"), ALU.add))
            link(dve.tensor_tensor(dest, pos, rows(base), ALU.add))
            for k, one in enumerate((one1, one2)):
                link(dve.tensor_tensor(pick_, pos, one, ALU.mult))
                link(dve.tensor_reduce(where[:, k], pick_, AX.X, ALU.add))
                link(dve.tensor_tensor(pick_, dest, one, ALU.mult))
                link(dve.tensor_reduce(place[:, k], pick_, AX.X, ALU.add))
            link(dve.tensor_scalar(inside, where, float(CAP), None, ALU.is_lt))
            wk = weigh_[:, 0:4].rearrange("p t e -> p (t e)").rearrange("p (k t) -> p k t", k=2)
            link(dve.tensor_tensor(m.route_weight, wk, inside, ALU.mult))
            link(dve.tensor_tensor(place, place, inside, ALU.mult))
            link(dve.tensor_copy(m.gather_at[:], place))
            link(dve.tensor_scalar(miss, inside, -float(4 * E_ * CAP), float(4 * E_ * CAP), ALU.mult, ALU.add))
            link(dve.tensor_tensor(miss, miss, place, ALU.add))
            dve.tensor_copy(m.scatter_at[:], miss)

PARTS = (5, 3)


def phase_shared(nc, m, part):
    RING = 8
    tag = f"f{part}_"
    blocks = PARTS[part]
    t0 = part * PARTS[0] * TT
    with ExitStack() as ctx:
        def sem(name):
            return ctx.enter_context(nc.semaphore(tag + name))

        def pb(name, shape):
            return ctx.enter_context(nc.psum_tensor(tag + name, shape, F32))

        a = Carver(m.arena2)
        silu = a.take(2, BT)
        hidden = a.take(2, len(FM), BT)
        base = a.take(2, TT, D)
        got = Carver(m.arena, m.odd_at).take(RING, 2, D)
        ps_g, ps_u, ps_d = pb("ps_g", [P, 2, BT]), pb("ps_u", [P, 2, BT]), pb("ps_d", [P, 2, 2 * D])
        scattered = sem("scattered") if part == 0 else None
        landed = [sem(f"landed{n}") for n in range(RING)] if part else None
        first, used, out_done = (sem("first"), sem("used"), sem("out_done")) if part else (None, None, None)
        out_dram = m.out.rearrange("a (t p) d -> p (a t) d", p=P)
        gu_done, silued, hid_made, d_done, based, summed = (sem("gu_done"), sem("silued"), sem("hid_made"), sem("d_done"),
                                                            sem("based"), sem("summed"))
        x_done = sem("x_done")
        nm = len(FM)
        block = ctx.enter_context(nc.Block())

        @block.tensor
        def _(pe):
            pe.sem_inc(d_done, 4)

            def up(b, s, h):
                rhs = [m.h_even[:, k, bass.ds(b * BT + t0 * P, BT)] for k in range(KC)]
                for i, (at, rows) in enumerate(FM):
                    pe.wait_ge(hid_made, nm * b + i + 1)
                    for ps, w in ((ps_g, m.s_gate), (ps_u, m.s_up)):
                        for k in range(KC):
                            last = pe.matmul(ps[0:rows, (s + i) % 2], w[:, k, at:at + rows], rhs[k], start=k == 0, stop=k == KC - 1)
                    last.then_inc(gu_done, 1)

            def down(b, s, h):
                pe.wait_ge(hid_made, nm * b + nm + 2)
                for c in range(2):
                    pe.wait_ge(summed, 2 * b + c + 1)
                    for t in range(2):
                        tok = (2 * c + t) * P
                        for i, (_, rows) in enumerate(FM):
                            last = pe.matmul(ps_d[:, c, t * D:t * D + D], hidden[0:rows, s, i, tok:tok + P], m.s_down[0:rows, i],
                                             start=i == 0, stop=i == nm - 1)
                    last.then_inc(d_done, 1)

            pipeline(pe, [(0, up), (1, down)], blocks)

        @block.scalar
        def _(act):
            def stage(b, s, h):
                for i, (at, rows) in enumerate(FM):
                    n = nm * b + i
                    act.wait_ge(gu_done, n + 1)
                    act.wait_ge(hid_made, n + 1)
                    act.activation(silu[0:rows, (s + i) % 2], ps_g[0:rows, (s + i) % 2], ACT.Silu).then_inc(silued, 1)

            pipeline(act, [(0, stage)], blocks)

        @block.vector
        def _(dve):
            dve.sem_inc(hid_made, 2)
            dve.sem_inc(summed, 2)
            dve.sem_inc(x_done, 2)

            def hide(b, s, h):
                dve.wait_ge(d_done, 2 * b + 2)
                for i, (at, rows) in enumerate(FM):
                    dve.wait_ge(silued, nm * b + i + 1)
                    dve.tensor_tensor(hidden[0:rows, s, i], ps_u[0:rows, (s + i) % 2], silu[0:rows, (s + i) % 2], ALU.mult)\
                       .then_inc(hid_made, 1)

            def add(b, s, h):
                dve.wait_ge(based, b + 3)
                for c in range(2):
                    dve.wait_ge(d_done, 2 * b + c + 5)
                    z = base[:, s, 2 * c:2 * c + 2]
                    dve.tensor_tensor(z, ps_d[:, c].rearrange("p (t n) -> p t n", t=2), z, ALU.add).then_inc(summed, 1)
                dve.wait_ge(summed, 2 * b + 4)
                x = m.x[:, bass.ds(b * TT + t0, TT)]
                dve.tensor_tensor(x, base[:, s], x, ALU.add).then_inc(x_done, 1)

            def take_experts(tiles):
                for t in tiles:
                    dve.wait_ge(landed[t % RING], 32 * (t // RING + 1))
                    x = m.x[:, t]
                    for k, done in enumerate((first, used)):
                        dve.scalar_tensor_tensor(x, got[:, t % RING, k], m.route_weight[:, k, t:t + 1], x, ALU.mult, ALU.add)\
                           .then_inc(done, 1)
                        if k == 0:
                            dve.wait_ge(first, t + 1)

            if part == 0:
                pipeline(dve, [(0, hide), (1, add)], blocks)
            else:
                for b in range(blocks):
                    hide(b, b % 2, b // 2)
                    if b:
                        add(b - 1, (b - 1) % 2, (b - 1) // 2)
                        dve.wait_ge(x_done, b + 2)
                    take_experts(range(8 * b, 8 * b + 8))
                add(blocks - 1, (blocks - 1) % 2, (blocks - 1) // 2)
                dve.wait_ge(x_done, blocks + 2)
                take_experts(range(8 * blocks, NT))

        @block.gpsimd
        def _(pool):
            pool.sem_inc(based, 2)

            def gate(b, s, h):
                hold(m, pool, x_done, b + 1)
                pool.tensor_tensor(base[:, s], m.h_rows[:, t0 + b * TT:t0 + b * TT + TT],
                                   m.gates[:, 1, 1:2].to_broadcast([P, TT, D]), ALU.mult).then_inc(based, 1)

            if part == 0:
                pool.wait_ge(m.zeroed, m.zeroed_expected)
            for b in range(blocks):
                gate(b, b % 2, b // 2)
                for t in range(b * NT // blocks, (b + 1) * NT // blocks):
                    if part and t >= RING:
                        pool.wait_ge(used, t - RING + 1)
                    for k in range(2):
                        if part == 0:
                            pool.indirect_dma_start(
                                out=m.slots_in[:, :], out_offset=bass.IndirectOffsetOnAxis(ap=m.scatter_at[:, k, t:t + 1], axis=0),
                                in_=m.h_rows[:, t], in_offset=None, bounds_check=E_ * CAP - 1, oob_is_err=False).then_inc(scattered, 16)
                        else:
                            pool.indirect_dma_start(
                                out=got[:, t % RING, k], out_offset=None, in_=m.slots_out[:, :],
                                in_offset=bass.IndirectOffsetOnAxis(ap=m.gather_at[:, k, t:t + 1], axis=0),
                                bounds_check=E_ * CAP - 1, oob_is_err=False).then_inc(landed[t % RING], 16)
            if part == 0:
                pool.wait_ge(scattered, 16 * 2 * NT)

        @block.sync
        def _(sp):
            if part:
                for t in range(0, NT, TT):
                    sp.wait_ge(used, t + TT)
                    sp.dma_start(out_dram[:, t:t + TT], m.x[:, t:t + TT]).then_inc(out_done, 16)
                sp.wait_ge(out_done, 16 * NB)


def phase_experts(nc, m):
    with ExitStack() as ctx:
        def sem(name):
            return ctx.enter_context(nc.semaphore("h_" + name))

        def pb(name, shape):
            return ctx.enter_context(nc.psum_tensor("h_" + name, shape, F32))

        HALF = CAP // 2
        a = Carver(m.arena, m.odd_at)
        w_gate, w_up = a.take(2, KC, FF), a.take(2, KC, FF)
        w_down = a.take(2, len(FM), D)
        rows_in = a.take(2, CT, D)
        rows_out = [a.take(CT, D)]
        a = Carver(m.arena2)
        rows_out.append(a.take(CT, D))
        inT = a.take(2, KC, CAP)
        silu = a.take(2, HALF)
        hidden = a.take(2, len(FM), CAP)
        ps_t = pb("ps_t", [P, 2, 2, 2 * P])
        ps_g, ps_u = pb("ps_g", [P, 2, BT]), pb("ps_u", [P, 2, BT])
        ps_d = pb("ps_d", [P, 2, BT])
        w_in = [sem("w_in0"), sem("w_in1")]
        wd_in = [sem("wd_in0"), sem("wd_in1")]
        x_in = [sem("x_in0"), sem("x_in1")]
        turned, taken, gu_done, silued, hid_made, d_done, kept = (sem("turned"), sem("taken"), sem("gu_done"), sem("silued"),
                                                                  sem("hid_made"), sem("d_done"), sem("kept"))
        stored = [sem("stored0"), sem("stored1")]
        folded = sem("folded")
        nm = len(FM)
        units = [(i, half) for i in range(nm) for half in range(2)]
        block = ctx.enter_context(nc.Block())

        def experts(eng, stages):
            top = max(sk for sk, _ in stages)
            start = top + top % 2

            def step(t, i=None):
                for sk, stage in stages:
                    e = t - sk
                    if i is not None:
                        stage(e + 2 * i, e % 2, e // 2 + i)
                    elif 0 <= e < E_:
                        stage(e, e % 2, e // 2)

            for t in range(start):
                step(t)
            pairs = (E_ - start) // 2
            with eng.Fori(0, pairs) as i:
                step(start, i)
                step(start + 1, i)
            for t in range(start + 2 * pairs, E_ + top):
                step(t)

        @block.sync
        def _(sp):
            for s in range(2):
                sp.sem_inc(stored[s], 16)

            def expert(ap, e):
                return ap[bass.ds(e, 1)]

            def load_rows(e, s, h):
                hold(m, sp, turned, CT * (e + 1))
                sp.dma_start(rows_in[:, s], m.slots_in[bass.ds(e * CAP, CAP), :].rearrange("(c p) n -> p c n", p=P)).then_inc(x_in[s], 16)

            def load_up(e, s, h):
                hold(m, sp, gu_done, 2 * nm * (e + 1))
                for dst, name in ((w_gate, "L1_ffn_w_gate"), (w_up, "L1_ffn_w_up")):
                    sp.dma_start(dst[:, s], expert(m.ins[name], e).rearrange("a (k p) n -> p (a k) n", p=P)).then_inc(w_in[s], 16)

            def load_down(e, s, h):
                hold(m, sp, d_done, CT * e + CT)
                src = expert(m.ins["L1_ffn_w_down"], e)
                sp.dma_start(w_down[:, s, 0:2], src[:, 0:2 * P].rearrange("a (k p) n -> p (a k) n", p=P)).then_inc(wd_in[s], 16)
                sp.dma_start(w_down[0:FF - 2 * P, s, 2], src[:, 2 * P:FF].rearrange("a p n -> p (a n)")).then_inc(wd_in[s], 16)

            def store(e, s, h):
                hold(m, sp, kept, CT * e + CT + 2)
                sp.dma_start(m.slots_out[bass.ds(e * CAP, CAP), :].rearrange("(c p) n -> p c n", p=P), rows_out[s]).then_inc(stored[s], 16)

            experts(sp, [(0, load_rows), (0, load_up), (1, load_down), (2, store)])
            for s in range(2):
                sp.wait_ge(stored[s], 16 * (E_ // 2 + 1))

        @block.tensor
        def _(pe):
            pe.sem_inc(d_done, 2 * CT)
            pe.sem_inc(turned, 2 * CT)
            pe.sem_inc(gu_done, 4 * nm)

            def turn(e, s, h):
                pe.wait_ge(x_in[s], 16 * (h + 1))
                for c in range(CT):
                    pe.wait_ge(taken, CT * e + c + 1)
                    for k in range(KC):
                        last = pe.transpose(ps_t[:, (s * CT + c) % 2, 0, k * P:k * P + P], rows_in[:, s, c, k * P:k * P + P], m.ident[:])
                    last.then_inc(turned, 1)

            def up(e, s, h):
                pe.wait_ge(w_in[s], 32 * (h + 1))
                pe.wait_ge(taken, CT * e + CT + 2)
                for n, (i, half) in enumerate(units):
                    at, rows = FM[i]
                    pe.wait_ge(hid_made, 2 * nm * e + n + 1)
                    for ps, w in ((ps_g, w_gate), (ps_u, w_up)):
                        for k in range(KC):
                            last = pe.matmul(ps[0:rows, n % 2, 0:HALF], w[:, s, k, at:at + rows],
                                             inT[:, s, k, half * HALF:half * HALF + HALF], start=k == 0, stop=k == KC - 1)
                    last.then_inc(gu_done, 1)

            def down(e, s, h):
                pe.wait_ge(hid_made, 2 * nm * e + 2 * nm + 2)
                pe.wait_ge(folded, e + 1)
                for c in range(CT):
                    pe.wait_ge(kept, CT * e + c + 1)
                    for i, (_, rows) in enumerate(FM):
                        last = pe.matmul(ps_d[:, (s * CT + c) % 2, 0:D], hidden[0:rows, s, i, c * P:c * P + P], w_down[0:rows, s, i],
                                         start=i == 0, stop=i == nm - 1)
                    last.then_inc(d_done, 1)

            experts(pe, [(0, turn), (0, up), (1, down)])

        @block.scalar
        def _(act):
            def gate(e, s, h):
                for n, (i, half) in enumerate(units):
                    rows = FM[i][1]
                    act.wait_ge(gu_done, 2 * nm * (e + 2) + n + 1)
                    act.activation(silu[0:rows, n % 2], ps_g[0:rows, n % 2, 0:HALF], ACT.Silu).then_inc(silued, 1)

            experts(act, [(0, gate)])

        @block.vector
        def _(dve):
            dve.sem_inc(hid_made, 2)
            dve.sem_inc(kept, 2)
            dve.sem_inc(taken, 2)

            def take(e, s, h):
                for c in range(CT):
                    dve.wait_ge(turned, CT * (e + 2) + c + 1)
                    dve.tensor_copy(inT[:, s, :, c * P:c * P + P], ps_t[:, (s * CT + c) % 2, 0].rearrange("p (k n) -> p k n", k=KC))\
                       .then_inc(taken, 1)

            def hide(e, s, h):
                for n, (i, half) in enumerate(units):
                    rows = FM[i][1]
                    dve.wait_ge(silued, 2 * nm * e + n + 1)
                    if n == 0:
                        dve.wait_ge(d_done, CT * e + CT)
                    dve.tensor_tensor(hidden[0:rows, s, i, half * HALF:half * HALF + HALF], ps_u[0:rows, n % 2, 0:HALF],
                                      silu[0:rows, n % 2], ALU.mult).then_inc(hid_made, 1)

            def keep_rows(e, s, h):
                dve.wait_ge(stored[s], 16 * (h + 1))
                for c in range(CT):
                    dve.wait_ge(d_done, CT * e + c + 1 + 2 * CT)
                    dve.tensor_copy(rows_out[s][:, c], ps_d[:, (s * CT + c) % 2, 0:D]).then_inc(kept, 1)

            experts(dve, [(0, take), (0, hide), (1, keep_rows)])

        @block.gpsimd
        def _(pool):
            def fold(e, s, h):
                hold(m, pool, wd_in[s], 32 * (h + 1))
                for i, (_, rows) in enumerate(FM):
                    last = pool.tensor_tensor(w_down[0:rows, s, i], w_down[0:rows, s, i], m.gates[0:rows, 1, 1], ALU.mult)
                last.then_inc(folded, 1)

            experts(pool, [(0, fold)])


def build(nc, ins, out):
    with ExitStack() as ctx:
        m = allocate(nc, ctx, ins, out)
        for phase in (phase_modulation, phase_project, phase_attend, phase_attend_unbounded, phase_weights, phase_attend_out,
                      phase_channel_mix, phase_delta, phase_route):
            phase(nc, m)
        phase_shared(nc, m, 0)
        phase_experts(nc, m)
        phase_shared(nc, m, 1)


def rope_table():
    inv_freq = (1.0 / np.float32(10000.0) ** (np.arange(0, DH, 2, dtype=np.float32) / np.float32(DH))).astype(np.float32)
    angle = np.arange(T, dtype=np.float32)[:, None] * inv_freq[None, :]
    cos, sin = np.cos(angle).T, np.sin(angle).T
    return np.stack([np.tile(np.concatenate([cos, cos]), (P // DH, 1)),
                     np.tile(np.concatenate([-sin, sin]), (P // DH, 1))]).astype(np.float32)


def constants():
    head = np.arange(P) // DH
    return {
        "ident": np.eye(P, dtype=np.float32),
        "rope": rope_table(),
        "head_ones": (head[:, None] == head[None, :]).astype(np.float32),
        "earlier": np.triu(np.ones((P, P), np.float32), 1),
        "keep_run": np.tile((np.arange(NT) > 0).astype(np.float32), (P, E_)),
        "backward": np.tile((E_ - np.arange(E_)).astype(np.float32), (P, 1)),
        "slot_base": np.tile((CAP * np.arange(E_)).astype(np.float32), (P, 1)),
        "zeros": np.zeros((1024, D), np.float32),
    }


def laid_out(inputs):
    qkv = inputs["L0_attn_qkv"]
    halves = np.arange(2 * D).reshape(-1, 2, DH // 2)[:, ::-1].reshape(-1)
    arrays = dict(inputs)
    arrays["qkvT"] = np.ascontiguousarray(qkv.T)
    arrays["qk_swapT"] = np.ascontiguousarray(qkv[halves].T)
    for name, source in (("woT", "L0_attn_wo"), ("W_rT", "L0_ffn_W_r"), ("W_kT", "L0_ffn_W_k"), ("W_vT", "L0_ffn_W_v")):
        arrays[name] = np.ascontiguousarray(inputs[source].T)
    arrays["b_beta_rep"] = np.repeat(inputs["L1_attn_b_beta"], DH)
    arrays.update(constants())
    return arrays


def kernel(**inputs):
    import concourse.bacc as bacc
    from concourse.bass_utils import run_bass_kernel_spmd

    nc = bacc.Bacc("TRN2", target_bir_lowering=False, num_devices=1)
    arrays = {n: np.ascontiguousarray(a) for n, a in laid_out({k: np.asarray(v) for k, v in inputs.items()}).items()}
    ins = {n: nc.dram_tensor("in_" + n, a.shape, mybir.dt.from_np(a.dtype), kind="ExternalInput").ap() for n, a in arrays.items()}
    out = nc.dram_tensor("out", (1, T, D), F32, kind="ExternalOutput").ap()
    build(nc, ins, out)
    r = run_bass_kernel_spmd(nc, [{"in_" + n: a for n, a in arrays.items()}], core_ids=[0])
    return r.results[0]["out"]
```
